# Optimizing a Trainium2 kernel written in Bass

```python
import numpy as np
import jax
import jax.numpy as jnp

def _softmax(x, axis=-1):
    return jax.nn.softmax(x, axis=axis)

def _gelu(x):
    return jax.nn.gelu(x, approximate=True)

def _silu(x):
    return jax.nn.silu(x)

def _sigmoid(x):
    return jax.nn.sigmoid(x)

def _layernorm(x, axis=-1, eps=1e-05):
    m = jnp.mean(x, axis=axis, keepdims=True)
    v = jnp.var(x, axis=axis, keepdims=True)
    return (x - m) / jnp.sqrt(v + eps)

def _scatter_add(tgt, idx, src, axis=0):
    return tgt.at[idx].add(src)

def _segment_sum(src, seg, n):
    return jax.ops.segment_sum(src, seg, n)
kernel_name = 'mk_flamingo_gated_d2_seqx_r4_e5d1b3'

def setup_inputs(seed: int=0):
    np.random.seed(seed)
    _w = jnp.asarray

    def _rec_inputs():
        import jax
        import jax.numpy as jnp
        _rk = jax.random.key(seed)
        x = -0.0003929 + 0.9999 * jax.random.normal(jax.random.fold_in(_rk, 1), (8, 100, 256), jnp.float32)
        _lenS = 100 - jax.random.randint(jax.random.fold_in(_rk, 7), (8,), 0, max(1, 100 // 4) + 1, jnp.int32)
        _lenS2 = 361 - jax.random.randint(jax.random.fold_in(_rk, 8), (8,), 0, max(1, 361 // 4) + 1, jnp.int32)
        _ctx_768P = jax.random.normal(jax.random.fold_in(_rk, 11), (8, 16, 192), jnp.float32)
        _ctx_768c = jax.random.dirichlet(jax.random.fold_in(_rk, 511), 0.3 * jnp.ones((16,), jnp.float32), (8, 361))
        _ctx_768t = jnp.einsum('bsk,bkd->bsd', _ctx_768c, _ctx_768P)
        _ctx_768t = _ctx_768t * jax.lax.rsqrt(jnp.mean(jnp.square(_ctx_768t)) + 1e-12) * 0.953939
        ctx_768 = -0.00055796 + 0.999787 * (_ctx_768t + 0.3 * jax.random.normal(jax.random.fold_in(_rk, 611), (8, 361, 192), jnp.float32))
        _g = jax.random.normal(jax.random.fold_in(_rk, 9001), (2, 2), jnp.float32)
        _g = jnp.sign(_g) * jnp.maximum(jnp.abs(_g), 1.0) + (_g == 0) * 1.0
        g_xattn = _g[0]
        g_ffn = _g[1]
        return (x, ctx_768, g_xattn, g_ffn)
    x, ctx_768, g_xattn, g_ffn = _rec_inputs()

    def _L0_xattn_setup():
        import jax, jax.numpy as jnp
        import numpy as np
        IMAGE_DIM = 256
        TEXT_DIM = 192
        NUM_HEADS = 16
        HEAD_DIM = IMAGE_DIM // NUM_HEADS
        key = jax.random.key(seed)
        ks = jax.random.split(key, 14)
        B, N, M = (4, 1024, 128)
        s_img = 1.0 / np.sqrt(IMAGE_DIM)
        s_txt = 1.0 / np.sqrt(TEXT_DIM)
        s_ff = 1.0 / np.sqrt(2 * IMAGE_DIM)
        return {'x': jax.random.normal(ks[0], (B, N, IMAGE_DIM), jnp.float32), 'y': jax.random.normal(ks[1], (B, M, TEXT_DIM), jnp.float32), 'Wq': jax.random.normal(ks[2], (IMAGE_DIM, IMAGE_DIM), jnp.float32) * s_img, 'bq': jax.random.normal(ks[3], (IMAGE_DIM,), jnp.float32) * s_img, 'Wk': jax.random.normal(ks[4], (TEXT_DIM, IMAGE_DIM), jnp.float32) * s_txt, 'bk': jax.random.normal(ks[5], (IMAGE_DIM,), jnp.float32) * s_txt, 'Wv': jax.random.normal(ks[6], (TEXT_DIM, IMAGE_DIM), jnp.float32) * s_txt, 'bv': jax.random.normal(ks[7], (IMAGE_DIM,), jnp.float32) * s_txt, 'W1': jax.random.normal(ks[8], (IMAGE_DIM, 2 * IMAGE_DIM), jnp.float32) * s_img, 'b1': jax.random.normal(ks[9], (2 * IMAGE_DIM,), jnp.float32) * s_img, 'W2': jax.random.normal(ks[10], (2 * IMAGE_DIM, IMAGE_DIM), jnp.float32) * s_ff, 'b2': jax.random.normal(ks[11], (IMAGE_DIM,), jnp.float32) * s_ff}
    _L0_xattn_all = _L0_xattn_setup()
    _L0_xattn_in = {k: v for k, v in _L0_xattn_all.items() if k in ('Wq', 'bq', 'Wk', 'bk', 'Wv', 'bv', 'W1', 'b1', 'W2', 'b2')}
    del _L0_xattn_all

    def _L0_ffn_setup():
        import jax, jax.numpy as jnp
        import numpy as np
        B, S, H, F, E = (2, 512, 256, 1024, 8)
        key = jax.random.key(seed)
        ks = jax.random.split(key, 4)
        x = jax.random.normal(ks[0], (B, S, H), dtype=jnp.float32)
        w_router = jax.random.normal(ks[1], (H, E), dtype=jnp.float32) * 0.02
        w1 = jax.random.normal(ks[2], (E, H, F), dtype=jnp.float32) * 0.02
        b1 = jnp.zeros((E, F), dtype=jnp.float32)
        w2 = jax.random.normal(ks[3], (E, F, H), dtype=jnp.float32) * 0.02
        b2 = jnp.zeros((E, H), dtype=jnp.float32)
        return {'x': x, 'w_router': w_router, 'w1': w1, 'b1': b1, 'w2': w2, 'b2': b2}
    _L0_ffn_all = _L0_ffn_setup()
    _L0_ffn_in = {k: v for k, v in _L0_ffn_all.items() if k in ('w_router', 'w1', 'b1', 'w2', 'b2')}
    del _L0_ffn_all

    def _L1_xattn_setup():
        import jax, jax.numpy as jnp
        import numpy as np
        import math
        E = 256
        EV = 256
        FFN = 1024
        DINO = 192
        B, S, P = (64, 128, 64)

        def bitnet_linear(x, W, b):
            w_scale = jnp.maximum(jnp.mean(jnp.abs(W)), 1e-05)
            qW = jnp.sign(W) * (jnp.abs(W) > 0.5 * w_scale).astype(W.dtype)
            i_scale = jnp.maximum(jnp.max(jnp.abs(x)), 1e-08) / 127.0
            qx = jnp.clip(jnp.round(x / i_scale), -128.0, 127.0)
            out = jnp.einsum('...i,oi->...o', qx, qW) * (w_scale * i_scale)
            return out + b
        key = jax.random.key(seed)
        ks = iter(jax.random.split(key, 32))

        def lin_w(fin, fout):
            return jax.random.normal(next(ks), (fout, fin), jnp.float32) * math.sqrt(2.0 / fin)
        return {'text_embeddings': jax.random.normal(next(ks), (B, S, E), jnp.float32), 'dinov2_features': jax.random.normal(next(ks), (B, P, DINO), jnp.float32), 'W_d2v': lin_w(DINO, EV), 'b_d2v': jnp.zeros((EV,), jnp.float32), 'W_img': lin_w(EV, E), 'b_img': jnp.zeros((E,), jnp.float32), 'W_txt': lin_w(E, E), 'b_txt': jnp.zeros((E,), jnp.float32), 'W_att0': lin_w(E, E // 2), 'b_att0': jnp.zeros((E // 2,), jnp.float32), 'W_att1': lin_w(E, E // 2), 'b_att1': jnp.zeros((E // 2,), jnp.float32), 'W_f1': lin_w(2 * E, FFN), 'b_f1': jnp.zeros((FFN,), jnp.float32), 'W_f2': lin_w(FFN, E), 'b_f2': jnp.zeros((E,), jnp.float32)}
    _L1_xattn_all = _L1_xattn_setup()
    _L1_xattn_in = {k: v for k, v in _L1_xattn_all.items() if k in ('W_d2v', 'b_d2v', 'W_img', 'b_img', 'W_txt', 'b_txt', 'W_att0', 'b_att0', 'W_att1', 'b_att1', 'W_f1', 'b_f1', 'W_f2', 'b_f2')}
    del _L1_xattn_all

    def _L1_ffn_setup():
        import jax, jax.numpy as jnp
        import numpy as np
        B, T, C, H, E, MIN_E = (4, 512, 256, 128, 16, 2)
        IS_CAUSAL = False

        def _forward(hidden_states, sim_matrix, gates, q_proj, k_proj, v_proj, o_proj):
            b, t, c = hidden_states.shape
            n = b * t
            x = hidden_states.reshape(n, c)
            xn = x / jnp.maximum(jnp.linalg.norm(x, axis=-1, keepdims=True), 1e-12)
            sn = sim_matrix / jnp.maximum(jnp.linalg.norm(sim_matrix, axis=0, keepdims=True), 1e-12)
            logits = xn @ sn - jax.nn.sigmoid(gates)
            gated = jax.nn.relu(logits)
            hard = (gated > 0).astype(gated.dtype)
            mask = gated + jax.lax.stop_gradient(hard - gated)
            inactive = jnp.sum(hard, axis=1) == 0
            _, fb_idx = jax.lax.top_k(logits, MIN_E)
            fb = jnp.zeros((n, logits.shape[1]), gated.dtype).at[jnp.arange(n)[:, None], fb_idx].set(1.0)
            put = jax.lax.stop_gradient(inactive[:, None].astype(gated.dtype) * fb)
            mask = mask * (1.0 - put) + put
            masked = jnp.where(mask > 0, gated, -jnp.inf)
            w = jax.nn.softmax(masked, axis=-1)

            def moe_proj(p):
                y = jnp.einsum('nc,ech->neh', x, p)
                return jnp.einsum('ne,neh->nh', w, y)
            q = moe_proj(q_proj).reshape(b, t, -1)
            k = moe_proj(k_proj).reshape(b, t, -1)
            v = moe_proj(v_proj).reshape(b, t, -1)
            h = q.shape[-1]
            scores = jnp.einsum('bth,bsh->bts', q, k) / jnp.sqrt(jnp.asarray(h, q.dtype))
            if IS_CAUSAL and t > 1:
                causal = jnp.tril(jnp.ones((t, t), bool))
                scores = jnp.where(causal[None], scores, -jnp.inf)
            attn = jax.nn.softmax(scores, axis=-1)
            o = jnp.einsum('bts,bsh->bth', attn, v).reshape(n, h)
            z = jnp.einsum('ne,nh->enh', w, o)
            out = jnp.einsum('enh,ehc->nc', z, o_proj)
            return out.reshape(b, t, c)
        key = jax.random.key(seed)
        ks = jax.random.split(key, 6)
        lim_qkv = float(np.sqrt(6.0 / (C + H)))
        inp = {'hidden_states': jax.random.normal(ks[0], (B, T, C), jnp.float32), 'sim_matrix': jax.random.normal(ks[1], (C, E), jnp.float32), 'gates': jnp.zeros((E,), jnp.float32), 'q_proj': jax.random.uniform(ks[2], (E, C, H), jnp.float32, -lim_qkv, lim_qkv), 'k_proj': jax.random.uniform(ks[3], (E, C, H), jnp.float32, -lim_qkv, lim_qkv), 'v_proj': jax.random.uniform(ks[4], (E, C, H), jnp.float32, -lim_qkv, lim_qkv), 'o_proj': jax.random.uniform(ks[5], (E, H, C), jnp.float32, -lim_qkv, lim_qkv)}
        return inp
    _L1_ffn_all = _L1_ffn_setup()
    _L1_ffn_in = {k: v for k, v in _L1_ffn_all.items() if k in ('sim_matrix', 'gates', 'q_proj', 'k_proj', 'v_proj', 'o_proj')}
    del _L1_ffn_all
    return {'x': x, 'ctx_768': ctx_768, 'g_xattn': g_xattn, 'g_ffn': g_ffn, 'L0_xattn_Wq': _L0_xattn_in['Wq'], 'L0_xattn_bq': _L0_xattn_in['bq'], 'L0_xattn_Wk': _L0_xattn_in['Wk'], 'L0_xattn_bk': _L0_xattn_in['bk'], 'L0_xattn_Wv': _L0_xattn_in['Wv'], 'L0_xattn_bv': _L0_xattn_in['bv'], 'L0_xattn_W1': _L0_xattn_in['W1'], 'L0_xattn_b1': _L0_xattn_in['b1'], 'L0_xattn_W2': _L0_xattn_in['W2'], 'L0_xattn_b2': _L0_xattn_in['b2'], 'L0_ffn_w_router': _L0_ffn_in['w_router'], 'L0_ffn_w1': _L0_ffn_in['w1'], 'L0_ffn_b1': _L0_ffn_in['b1'], 'L0_ffn_w2': _L0_ffn_in['w2'], 'L0_ffn_b2': _L0_ffn_in['b2'], 'L1_xattn_W_d2v': _L1_xattn_in['W_d2v'], 'L1_xattn_b_d2v': _L1_xattn_in['b_d2v'], 'L1_xattn_W_img': _L1_xattn_in['W_img'], 'L1_xattn_b_img': _L1_xattn_in['b_img'], 'L1_xattn_W_txt': _L1_xattn_in['W_txt'], 'L1_xattn_b_txt': _L1_xattn_in['b_txt'], 'L1_xattn_W_att0': _L1_xattn_in['W_att0'], 'L1_xattn_b_att0': _L1_xattn_in['b_att0'], 'L1_xattn_W_att1': _L1_xattn_in['W_att1'], 'L1_xattn_b_att1': _L1_xattn_in['b_att1'], 'L1_xattn_W_f1': _L1_xattn_in['W_f1'], 'L1_xattn_b_f1': _L1_xattn_in['b_f1'], 'L1_xattn_W_f2': _L1_xattn_in['W_f2'], 'L1_xattn_b_f2': _L1_xattn_in['b_f2'], 'L1_ffn_sim_matrix': _L1_ffn_in['sim_matrix'], 'L1_ffn_gates': _L1_ffn_in['gates'], 'L1_ffn_q_proj': _L1_ffn_in['q_proj'], 'L1_ffn_k_proj': _L1_ffn_in['k_proj'], 'L1_ffn_v_proj': _L1_ffn_in['v_proj'], 'L1_ffn_o_proj': _L1_ffn_in['o_proj']}

def reference(x, ctx_768, g_xattn, g_ffn, L0_xattn_Wq, L0_xattn_bq, L0_xattn_Wk, L0_xattn_bk, L0_xattn_Wv, L0_xattn_bv, L0_xattn_W1, L0_xattn_b1, L0_xattn_W2, L0_xattn_b2, L0_ffn_w_router, L0_ffn_w1, L0_ffn_b1, L0_ffn_w2, L0_ffn_b2, L1_xattn_W_d2v, L1_xattn_b_d2v, L1_xattn_W_img, L1_xattn_b_img, L1_xattn_W_txt, L1_xattn_b_txt, L1_xattn_W_att0, L1_xattn_b_att0, L1_xattn_W_att1, L1_xattn_b_att1, L1_xattn_W_f1, L1_xattn_b_f1, L1_xattn_W_f2, L1_xattn_b_f2, L1_ffn_sim_matrix, L1_ffn_gates, L1_ffn_q_proj, L1_ffn_k_proj, L1_ffn_v_proj, L1_ffn_o_proj):
    import jax
    import jax.numpy as jnp

    def _L0_xattn_ref(x, y, Wq, bq, Wk, bk, Wv, bv, W1, b1, W2, b2):
        import jax, jax.numpy as jnp
        import numpy as np
        IMAGE_DIM = 256
        TEXT_DIM = 192
        NUM_HEADS = 16
        HEAD_DIM = IMAGE_DIM // NUM_HEADS
        B, N, _ = x.shape
        M = y.shape[1]
        q = (x @ Wq + bq).reshape(B, N, NUM_HEADS, HEAD_DIM)
        k = (y @ Wk + bk).reshape(B, M, NUM_HEADS, HEAD_DIM)
        v = (y @ Wv + bv).reshape(B, M, NUM_HEADS, HEAD_DIM)
        scale = 1.0 / np.sqrt(HEAD_DIM)
        scores = jnp.einsum('bnhd,bmhd->bhnm', q, k) * scale
        attn = jax.nn.softmax(scores, axis=-1)
        out = jnp.einsum('bhnm,bmhd->bnhd', attn, v).reshape(B, N, IMAGE_DIM)
        h = jax.nn.relu(out @ W1 + b1)
        return h @ W2 + b2

    def _L0_ffn_ref(x, w_router, w1, b1, w2, b2):
        import jax, jax.numpy as jnp
        import numpy as np
        B, S, H, F, E = (2, 512, 256, 1024, 8)
        'Top-1 MoE layer: route -> per-expert FFN -> weighted combine.\n\n            Faithful to ExpertParallelWrapper._process_moe_layer on a single group:\n            router picks one expert per token with a routing weight; tokens are\n            dispatched to experts (here expressed as a static mask over the fixed\n            expert set), processed by the expert FFN, and scatter-combined back\n            weighted by the routing probability.\n            '
        Bs, Ss, Hs = x.shape
        n_experts = w1.shape[0]
        logits = jnp.einsum('bsh,he->bse', x, w_router)
        probs = jax.nn.softmax(logits, axis=-1)
        sel = jnp.argmax(probs, axis=-1)
        wgt = jnp.take_along_axis(probs, sel[..., None], axis=-1)[..., 0]
        xt = x.reshape(-1, Hs)
        sel_t = sel.reshape(-1)
        wgt_t = wgt.reshape(-1)
        out = jnp.zeros_like(xt)
        for e in range(n_experts):
            h = jax.nn.relu(xt @ w1[e] + b1[e])
            y = h @ w2[e] + b2[e]
            m = (sel_t == e).astype(xt.dtype) * wgt_t
            out = out + m[:, None] * y
        return out.reshape(Bs, Ss, Hs)

    def _L1_xattn_ref(text_embeddings, dinov2_features, W_d2v, b_d2v, W_img, b_img, W_txt, b_txt, W_att0, b_att0, W_att1, b_att1, W_f1, b_f1, W_f2, b_f2):
        import jax, jax.numpy as jnp
        import numpy as np
        import math
        E = 256
        EV = 256
        FFN = 1024
        DINO = 192
        B, S, P = (64, 128, 64)

        def bitnet_linear(x, W, b):
            w_scale = jnp.maximum(jnp.mean(jnp.abs(W)), 1e-05)
            qW = jnp.sign(W) * (jnp.abs(W) > 0.5 * w_scale).astype(W.dtype)
            i_scale = jnp.maximum(jnp.max(jnp.abs(x)), 1e-08) / 127.0
            qx = jnp.clip(jnp.round(x / i_scale), -128.0, 127.0)
            out = jnp.einsum('...i,oi->...o', qx, qW) * (w_scale * i_scale)
            return out + b
        b, s, e = text_embeddings.shape
        vis = bitnet_linear(dinov2_features, W_d2v, b_d2v)
        image_embeds = bitnet_linear(vis, W_img, b_img)
        fused = bitnet_linear(text_embeddings, W_txt, b_txt)
        inv_sqrt_e = 1.0 / math.sqrt(e)
        for Wa, ba in ((W_att0, b_att0), (W_att1, b_att1)):
            kv = bitnet_linear(image_embeds, Wa, ba)
            k = jnp.concatenate([kv, kv], axis=-1)
            scores = jnp.einsum('bse,bpe->bsp', fused, k) * inv_sqrt_e
            attn = jax.nn.softmax(scores, axis=-1)
            fused = fused + 0.1 * jnp.einsum('bsp,bpe->bse', attn, k)
        avg_img = jnp.mean(image_embeds, axis=1, keepdims=True)
        concatenated = jnp.concatenate([fused, jnp.broadcast_to(avg_img, (b, s, e))], axis=-1)
        h = jax.nn.relu(bitnet_linear(concatenated, W_f1, b_f1))
        return bitnet_linear(h, W_f2, b_f2)

    def _L1_ffn_ref(hidden_states, sim_matrix, gates, q_proj, k_proj, v_proj, o_proj):
        import jax, jax.numpy as jnp
        import numpy as np
        B, T, C, H, E, MIN_E = (4, 512, 256, 128, 16, 2)
        IS_CAUSAL = False

        def _forward(hidden_states, sim_matrix, gates, q_proj, k_proj, v_proj, o_proj):
            b, t, c = hidden_states.shape
            n = b * t
            x = hidden_states.reshape(n, c)
            xn = x / jnp.maximum(jnp.linalg.norm(x, axis=-1, keepdims=True), 1e-12)
            sn = sim_matrix / jnp.maximum(jnp.linalg.norm(sim_matrix, axis=0, keepdims=True), 1e-12)
            logits = xn @ sn - jax.nn.sigmoid(gates)
            gated = jax.nn.relu(logits)
            hard = (gated > 0).astype(gated.dtype)
            mask = gated + jax.lax.stop_gradient(hard - gated)
            inactive = jnp.sum(hard, axis=1) == 0
            _, fb_idx = jax.lax.top_k(logits, MIN_E)
            fb = jnp.zeros((n, logits.shape[1]), gated.dtype).at[jnp.arange(n)[:, None], fb_idx].set(1.0)
            put = jax.lax.stop_gradient(inactive[:, None].astype(gated.dtype) * fb)
            mask = mask * (1.0 - put) + put
            masked = jnp.where(mask > 0, gated, -jnp.inf)
            w = jax.nn.softmax(masked, axis=-1)

            def moe_proj(p):
                y = jnp.einsum('nc,ech->neh', x, p)
                return jnp.einsum('ne,neh->nh', w, y)
            q = moe_proj(q_proj).reshape(b, t, -1)
            k = moe_proj(k_proj).reshape(b, t, -1)
            v = moe_proj(v_proj).reshape(b, t, -1)
            h = q.shape[-1]
            scores = jnp.einsum('bth,bsh->bts', q, k) / jnp.sqrt(jnp.asarray(h, q.dtype))
            if IS_CAUSAL and t > 1:
                causal = jnp.tril(jnp.ones((t, t), bool))
                scores = jnp.where(causal[None], scores, -jnp.inf)
            attn = jax.nn.softmax(scores, axis=-1)
            o = jnp.einsum('bts,bsh->bth', attn, v).reshape(n, h)
            z = jnp.einsum('ne,nh->enh', w, o)
            out = jnp.einsum('enh,ehc->nc', z, o_proj)
            return out.reshape(b, t, c)
        return _forward(hidden_states, sim_matrix, gates, q_proj, k_proj, v_proj, o_proj)
    x = x + jnp.tanh(g_xattn[0]) * _L0_xattn_ref(_layernorm(x, axis=-1), ctx_768, L0_xattn_Wq, L0_xattn_bq, L0_xattn_Wk, L0_xattn_bk, L0_xattn_Wv, L0_xattn_bv, L0_xattn_W1, L0_xattn_b1, L0_xattn_W2, L0_xattn_b2)
    x = x + jnp.tanh(g_ffn[0]) * _L0_ffn_ref(_layernorm(x, axis=-1), L0_ffn_w_router, L0_ffn_w1, L0_ffn_b1, L0_ffn_w2, L0_ffn_b2)
    x = x + jnp.tanh(g_xattn[1]) * _L1_xattn_ref(_layernorm(x, axis=-1), ctx_768, L1_xattn_W_d2v, L1_xattn_b_d2v, L1_xattn_W_img, L1_xattn_b_img, L1_xattn_W_txt, L1_xattn_b_txt, L1_xattn_W_att0, L1_xattn_b_att0, L1_xattn_W_att1, L1_xattn_b_att1, L1_xattn_W_f1, L1_xattn_b_f1, L1_xattn_W_f2, L1_xattn_b_f2)
    x = x + jnp.tanh(g_ffn[1]) * _L1_ffn_ref(_layernorm(x, axis=-1), L1_ffn_sim_matrix, L1_ffn_gates, L1_ffn_q_proj, L1_ffn_k_proj, L1_ffn_v_proj, L1_ffn_o_proj)
    return x

_drawn_inputs = setup_inputs


def setup_inputs(seed=0):
    import zlib

    import numpy as np

    out = dict(_drawn_inputs(seed))
    spreads = {'g_ffn': (-1.0, 0.6),
     'L0_ffn_b1': (0.0, 0.514),
     'L0_ffn_b2': (0.0, 0.388),
     'L1_xattn_b_d2v': (0.0, 0.1),
     'L1_xattn_b_img': (0.0, 0.1),
     'L1_xattn_b_txt': (0.0, 0.1),
     'L1_xattn_b_att0': (0.0, 1.682),
     'L1_xattn_b_att1': (0.0, 1.843),
     'L1_xattn_b_f1': (0.0, 0.1),
     'L1_xattn_b_f2': (0.0, 0.1),
     'L1_ffn_gates': (0.0, 0.1)}
    factors = {'L0_xattn_bq': 4.17, 'L0_xattn_bk': 64.0, 'L1_xattn_W_att0': 2.769}
    for name, (base, spread) in spreads.items():
        noise = np.random.default_rng([zlib.crc32(name.encode()), seed]).standard_normal(out[name].shape)
        drawn = base * np.exp(spread * noise) if base else spread * noise
        out[name] = jnp.asarray(drawn.astype(out[name].dtype))
    for name, factor in factors.items():
        out[name] = (out[name] * factor).astype(out[name].dtype)
    return out
```

```python
from contextlib import ExitStack

import concourse.bass as bass
import numpy as np
from concourse import mybir

ALU = mybir.AluOpType
ACT = mybir.ActivationFunctionType
AX = mybir.AxisListType
F32 = mybir.dt.float32
BF16 = mybir.dt.bfloat16
I32 = mybir.dt.int32
U32 = mybir.dt.uint32
RMAX = bass.bass_isa.ReduceOp.max
RADD = bass.bass_isa.ReduceOp.add

P = 128
B, N, D = 8, 100, 256
T = B * N
HT = T // 2
M, DT = 361, 192
KC = DT // 2
H, HD = 16, 16
CH = [(0, 121), (121, 121), (242, 119)]
CW = 121
F0 = 512
E0, FE = 8, 1024
KF = FE // P
SLOTS = P
OVER = T // SLOTS
TILES = E0 + OVER
E1, HE = 16, 128
BIT_F = 1024
STAGE = 13004
ORDER = [8 * t + 2 * g + q for t in range(2) for q in range(2) for g in range(4)]
OWN = (0, 3, 6)
MAGIC = 12582912.0
EPS = 1e-5
BIG = 1e30

CONST = {}
_at = 0
for _name, _w in (("ident", P), ("ones", P), ("before", N), ("headmask", 8), ("lower", E0 * E0),
                  ("bounds", OVER), ("base", E0), ("rev8", E0), ("rev16", E1), ("over", OVER),
                  ("spread", 2 * P)):
    CONST[_name] = (_at, _at + _w)
    _at += _w
CONST_W = _at

COLS = {"bq": 0, "bk": 2, "b1": 4, "d2v": 8, "img": 10, "att": 12, "txt": 14, "f1": 16}
COLS_W = 26
ROWS = {"bv": (0, 256), "b2": (256, 512), "att": (512, 768), "f2": (768, 1024),
        "gates": (1024, 1040), "gx": (1040, 1042), "gf": (1042, 1044)}
ROWS_W = 1044

TERN = {}
_at = 0
for _name, _p, _w in (("d2v", KC, 512), ("img", P, 512), ("txt", P, 512), ("att0", P, 256),
                      ("att1", P, 256), ("f1", P, 4096), ("f2", P, 2048)):
    TERN[_name] = (_p, _w, _at)
    _at += _w
TERN_W = _at
TERN_NAMES = list(TERN)


def shape_constants():
    c = np.zeros((P, CONST_W), np.float32)

    def put(name, value):
        a, b = CONST[name]
        c[:, a:b][:value.shape[0]] = value

    i = np.arange(P)
    put("ident", np.eye(P, dtype=np.float32))
    put("ones", np.ones((P, P), np.float32))
    put("before", (i[:N, None] < i[None, :N]).astype(np.float32))
    put("headmask", (i[:, None] // HD == i[None, :8]).astype(np.float32))
    e = np.arange(E0)
    put("lower", np.tile((e[None, :] < e[:, None]).astype(np.float32).reshape(1, -1), (P, 1)))
    put("bounds", np.tile(np.arange(1, OVER + 1, dtype=np.float32) * SLOTS, (P, 1)))
    put("base", np.tile(e.astype(np.float32) * SLOTS, (P, 1)))
    put("rev8", np.tile((E0 - e).astype(np.float32), (P, 1)))
    put("rev16", np.tile((E1 - np.arange(E1)).astype(np.float32), (P, 1)))
    put("over", np.tile(np.arange(OVER, dtype=np.float32), (P, 1)))
    put("spread", (np.arange(2 * P)[None, :] // HD == np.arange(H)[:, None]).astype(np.float32))
    return c


def flamingo(nc, d):
    ctx = ExitStack()
    with ctx:
        def sb(name, shape, dt=F32):
            return ctx.enter_context(nc.sbuf_tensor(name, shape, dt))

        def sem(name):
            return ctx.enter_context(nc.semaphore(name))

        consts = sb("consts", [P, CONST_W])
        cols = sb("cols", [P, COLS_W])
        rows = sb("rows", [P, ROWS_W])
        tern = sb("tern", [P, TERN_W], BF16)
        x = sb("x", [N, B, D])
        xn_region = sb("xn", [P, B * D])
        xn = xn_region[0:N, :].rearrange("p (b d) -> p b d", b=B)
        xT = sb("xT", [P, 2, T])
        ws = sb("ws", [P, 2, 7])
        wabs = sb("wabs", [P, 14])
        scol = sb("scol", [P, 64])
        kvT = sb("kvT", [P, 2, B, M])
        kvt = sb("kvt", [CW, 3, B, 2, P])
        avg = sb("avg", [P, 2, B])
        w_a = sb("w_a", [P, 1552])
        stats = sb("stats", [N, B, 6])
        tile_expert = sb("tile_expert", [1, OVER], I32)
        slot_of = sb("slot_of", [N, B], U32)
        region = sb("region", [P, 11552])
        stage = sb("stage", [P, STAGE])
        psum = [ctx.enter_context(nc.psum_tensor(f"bank{i}", [P, 512], F32)) for i in range(8)]

        def const(name, n=P):
            a, b = CONST[name]
            return consts[0:n, a:b]

        ident = const("ident")
        raw = stage[:, 0:TERN_W]

        def weight(name):
            p, w, at = TERN[name]
            return tern[0:p, at:at + w]

        ctx_a = region[:, 0:5776].rearrange("p (k b m) -> p k b m", k=2, b=B)
        qa = region[:, 5776:8664].bitcast(BF16).rearrange("p (k b m) -> p k b m", k=2, b=B)
        qb = region[:, 8664:11552].bitcast(BF16).rearrange("p (k b m) -> p k b m", k=2, b=B)

        at = [0]

        def cut(n):
            at[0] += n
            return stage[:, at[0] - n:at[0]]

        ctx_b = [cut(2 * M)[0:KC].rearrange("p (k m) -> p k m", k=2) for _ in range(2)]
        k_b = [cut(2 * M).rearrange("p (k m) -> p k m", k=2) for _ in range(2)]
        v_b = [cut(3 * H * 32)[0:CW].rearrange("p (c h w) -> p c h w", c=3, h=H) for _ in range(2)]
        q_b = [cut(H * N).rearrange("p (h n) -> p h n", h=H) for _ in range(2)]
        probs = [cut(M)[0:N] for _ in range(4)]
        probsT = [cut(3 * N)[0:CW] for _ in range(8)]
        assert at[0] <= STAGE
        qT = xn_region[:, 0:2 * T].rearrange("p (k t) -> p k t", k=2)
        sumT = stage[0:H, 0:T]
        h0T = stage[:, 1000:1000 + 4 * T].rearrange("p (m t) -> p m t", m=4)
        w_q = w_a[:, 0:512].rearrange("p (k n) -> p k n", k=2)
        w_k = w_a[0:KC, 512:1024].rearrange("p (k n) -> p k n", k=2)
        w_v = w_a[0:KC, 1024:1536].rearrange("p (k n) -> p k n", k=2)
        w_r = w_a[:, 1536:1552].rearrange("p (k n) -> p k n", k=2)
        w_1 = region[:, 5776:6800].rearrange("p (k n) -> p k n", k=2)
        w_2 = region[:, 6800:7824].rearrange("p (k n) -> p k n", k=4)
        e_w1 = [region[:, u * 2048:(u + 1) * 2048].rearrange("p (k n) -> p k n", k=2) for u in range(2)]
        e_w2 = [region[:, 4096 + u * 2048:4096 + (u + 1) * 2048].rearrange("p (k n) -> p k n", k=KF)
                for u in range(2)]
        at[0] = 4400
        e_b1 = [cut(KF) for _ in range(2)]
        e_b2 = [cut(D) for _ in range(2)]
        xs = [cut(D) for _ in range(2)]
        xsT = [cut(D).rearrange("p (k s) -> p k s", k=2) for _ in range(2)]
        hsT = [cut(KF * SLOTS).rearrange("p (m s) -> p m s", m=KF) for _ in range(2)]
        ys = [cut(D) for _ in range(2)]
        y_tok = cut(B * D)[0:N].rearrange("p (b n) -> p b n", b=B)
        at[0] = 0
        qx = cut(T).bitcast(BF16).rearrange("p (k t) -> p k t", k=2)
        fT = cut(2 * T).rearrange("p (k t) -> p k t", k=2)
        fsum = cut(T)
        bprobs = [cut(M)[0:N] for _ in range(3)]
        bprobsT = [cut(3 * N)[0:CW] for _ in range(2)]
        qavg = cut(B).bitcast(BF16).rearrange("p (k b) -> p k b", k=2)
        q_tmp = cut(2 * T)
        h1T = region[:, 0:8 * T].rearrange("p (m t) -> p m t", m=8)
        q1T = region[:, 8 * T:8 * T + 4 * T].bitcast(BF16).rearrange("p (m t) -> p m t", m=8)
        at[0] = 0
        x_w = [cut(2 * T).rearrange("p (k t) -> p k t", k=2) for _ in range(2)]
        w_bc = [cut(T) for _ in range(2)]
        p_w = [cut(2 * 3 * HE).rearrange("p (k n) -> p k n", k=2) for _ in range(2)]
        o_w = [cut(D) for _ in range(2)]
        z_w = [cut(T) for _ in range(2)]
        at_r = [0]

        def cut_r(n):
            at_r[0] += n
            return region[:, at_r[0] - n:at_r[0]]

        qkvT = [cut_r(T) for _ in range(3)]
        v_tok = cut_r(B * HE)[0:N].rearrange("p (b h) -> p b h", b=B)
        lprobs = [cut_r(N)[0:N] for _ in range(B)]
        lprobsT = [cut_r(N)[0:N] for _ in range(B)]
        oT = cut_r(T)
        yT = cut_r(2 * T).rearrange("p (k t) -> p k t", k=2)
        wT = cut_r(T)[0:E1]
        square = cut_r(B * D)[0:N].rearrange("p (b d) -> p b d", b=B)
        assert at_r[0] <= 11552 and at[0] <= STAGE

        mv = sb("mv", [N, B, 2])
        var = sb("var", [N, B])
        std = sb("std", [N, B])
        rstd = sb("rstd", [N, B])
        nmax = sb("nmax", [N, 2, H])
        psums = sb("psums", [N, B, H])
        precip = sb("precip", [N, B, H])
        tg = sb("tg", [P, 4])
        tmp256 = sb("tmp256", [N, 2, D])
        lg = sb("lg", [N, B, E1])
        l_a = sb("l_a", [N, B, E1])
        l_b = sb("l_b", [N, B, E1])
        l_c = sb("l_c", [N, B, E1])
        l_d = sb("l_d", [N, B, E1])
        l_c2 = sb("l_c2", [N, B, E1])
        r_a = sb("r_a", [N, B])
        r_b = sb("r_b", [N, B])
        r_c = sb("r_c", [N, B])
        onehot = sb("onehot", [N, B, E0])
        seen = sb("seen", [N, B + 1, E0])
        rank = sb("rank", [N, B, E0])
        ex_a = sb("ex_a", [N, E0, E0])
        extra = sb("extra", [N, E0])
        extra_base = sb("extra_base", [N, E0])
        count = sb("count", [N, E0])
        te = sb("te", [N, OVER])
        top_w = sb("top_w", [N, B])
        umax = sb("umax", [P, 16])
        sim = sb("sim", [P, 2, E1])
        simsq = sb("simsq", [P, 2, E1])
        simn = sb("simn", [N, E1])
        sig = sb("sig", [N, E1])
        nsq = sb("nsq", [N, B])
        zero_tile = sb("zero_tile", [P, D])

        S = {n: sem(n) for n in (
            "small_in", "x_in", "raw_in", "ctx_half_in0", "ctx_half_in1", "ffn_in", "w_abs", "w_abs_all", "tern_ready",
            "ln_var", "ln_std", "ln_out", "ln_turned", "xT_ready",
            "max_part", "max_all", "quantised", "layer_mm", "layer_out", "kv_mm", "kv_out", 
            "q_mm", "q_out", "ctx_in0", "ctx_in1", "q_spread", "proj_mm", "k_out", "v_out",
            "scores_mm", "max_out", "exp_out", "turned", "turn_out", "pv_mm", "o_out",
            "norm_a", "norm_mm", "norm_b", "h0_mm", "h0_out", "y0_mm", "x1_done",
            "logit_mm", "logit_a", "logit_e", "onehot_done", "rank_mm", "slot_done", "te_done", "zeroed",
            "scattered", "w1_in0", "w1_in1", "w2_in0", "w2_in1", "xs_in0", "xs_in1", "xs_turned", "xs_out",
            "h_mm", "h_out_a", "h_out_v", "y_mm", "y_out", "y_stored0", "y_stored1", "y_free", "gathered0", "gathered1", "gathered2", "gathered3", "x2_done",
            "txt_mm", "txt_out", "fsum_done", "bs_mm", "bmax", "bexp", "bnorm", "bturned", "bturn_out",
            "bpv_mm", "f_done", "f1_mm", "f1_out", "q1_done", "f2_mm", "h1_scale", "h1_scaled", "x3_done",
            "sq_done", "simsq_done", "simn_mm", "lg_mm", "lg_act", "lg_vec", "w_done", "wT_mm", "wT_out",
            "wT_stored", "w0_mm", "p_in0", "p_in1", "wb_in0", "wb_in1", "xw_done", "qkv_mm", "qkv_out",
            "vt_mm", "vt_out", "ls_mm", "lmax", "lexp", "lnorm", "lturned", "lturn_out", "lpv_mm", "o_ready",
            "o_in0", "o_in1", "wz_in0", "wz_in1", "z_done", "out_mm", "yT_out", "y_turned", "x4_done",
            "out_stored", "dve_step", "act_step", "gates_done", "unit_max", "thresholds", "pool_step", "below_done", "v_zeroed", "large_in", "large_abs", "norm_b2", "zero_tile_set")}
        block = ctx.enter_context(nc.Block())

        def values(pe, i, u, g4):
            pe.wait_ge(S["turn_out"], i * 32 + (16 * u + 2 + 4 * g4 + 4))
            if g4 == 0:
                pe.wait_ge(S["o_out"], i * 2 + (u + 1))
            for c, (_, rows_c) in enumerate(CH):
                for g in range(4):
                    j = 4 * g4 + g
                    head = ORDER[j]
                    t, odd = head // 8, head % 2
                    ins = pe.matmul(psum[5 + u][32 * g:32 * g + 32, t * N:(t + 1) * N],
                                    v_b[u][0:rows_c, c, head, :], probsT[j % 8][0:rows_c, c * N:(c + 1) * N],
                                    start=odd == 0 and c == 0, stop=odd == 1 and c == 2)
            ins.then_inc(S["pv_mm"], 1)

        def add_out(dve, a, b):
            dve.wait_ge(S["bpv_mm"], B * a + b + 1)
            dst = fT[:, :, b * N:(b + 1) * N]
            dve.scalar_tensor_tensor(dst, psum[5 + b % 2][:, None, 0:N].to_broadcast([P, 2, N]), 0.1, dst,
                                     ALU.mult, ALU.add).then_inc(S["f_done"], 1)

        @block.sync
        def _(sp):
            for h in range(2):
                sp.dma_start(ctx_a[0:KC, :, 4 * h:4 * h + 4], d["ctxT"][:, :, 4 * h:4 * h + 4])\
                    .then_inc(S[f"ctx_half_in{h}"], 16)
            sp.dma_start(consts[:, :], d["consts"]).then_inc(S["small_in"], 16)
            sp.dma_start(cols[:, 0:24], d["cols"]).then_inc(S["small_in"], 16)
            sp.dma_start(rows[:, :], d["rows"].to_broadcast([P, ROWS_W])).then_inc(S["small_in"], 16)
            sp.dma_start(w_a[:, :], d["w_a"]).then_inc(S["small_in"], 16)
            sp.dma_start(sim[:, :, :], d["sim"]).then_inc(S["small_in"], 16)

            sp.wait_ge(S["tern_ready"], 7)
            for u in range(2):
                sp.dma_start(ctx_b[u], d["ctxT"][:, :, u, :]).then_inc(S[f"ctx_in{u}"], 16)
            with sp.Fori(1, B // 2) as i:
                for u in range(2):
                    sp.wait_ge(S["proj_mm"], i * 10 + (5 * u - 5))
                    sp.dma_start(ctx_b[u], d["ctxT"][:, :, i * 2 + u, :]).then_inc(S[f"ctx_in{u}"], 16)
            sp.wait_ge(S["quantised"], 2)
            sp.dma_start(w_1, d["w_1"]).then_inc(S["ffn_in"], 16)
            sp.dma_start(w_2, d["w_2"]).then_inc(S["ffn_in"], 16)

            def load_expert(u, e):
                sp.dma_start(e_w1[u], d["e_w1"][e]).then_inc(S[f"w1_in{u}"], 16)

            def load_expert_2(u, e):
                sp.dma_start(e_w2[u], d["e_w2"][e]).then_inc(S[f"w2_in{u}"], 16)

            def load_bias(u, e):
                sp.dma_start(e_b1[u], d["e_b1"][e]).then_inc(S[f"w2_in{u}"], 16)
                sp.dma_start(e_b2[u], d["e_b2"][bass.ds(e, 1), :].to_broadcast([P, D])).then_inc(S[f"w2_in{u}"], 16)

            sp.wait_ge(S["quantised"], 3)
            for u in range(2):
                load_expert(u, u)
            sp.wait_ge(S["x1_done"], B)
            for u in range(2):
                load_expert_2(u, u)
                load_bias(u, u)

            def reload(u, t, e):
                sp.wait_ge(S["h_mm"], t * 2 - 2)
                load_expert(u, e)
                sp.wait_ge(S["y_mm"], t - 1)
                load_expert_2(u, e)
                sp.wait_ge(S["y_out"], t + 1)
                load_bias(u, e)

            with sp.Fori(1, E0 // 2) as i:
                for u in range(2):
                    reload(u, i * 2 + u, i * 2 + u)
            sp.wait_ge(S["te_done"], 1)
            with sp.Fori(0, OVER // 2) as i:
                for u in range(2):
                    e = sp.value_load(tile_expert[0:1, bass.ds(i * 2 + u, 1)], min_val=0, max_val=E0 - 1)
                    reload(u, i * 2 + (E0 + u), e)

            def load_weights(u, e):
                sp.dma_start(w_bc[u], d["w_dram"][bass.ds(e, 1), :].to_broadcast([P, T])).then_inc(S[f"wb_in{u}"], 16)

            def load_proj(u, e):
                sp.dma_start(p_w[u], d["p_qkv"][e]).then_inc(S[f"p_in{u}"], 16)

            sp.wait_ge(S["f2_mm"], 1)
            for u in range(2):
                load_proj(u, u)
            sp.wait_ge(S["wT_out"], 2)
            sp.dma_start(d["w_dram"], wT).then_inc(S["wT_stored"], 16)
            sp.wait_ge(S["wT_stored"], 16)
            load_weights(1, 1)
            with sp.Fori(1, E1 // 2) as i:
                for u in range(2):
                    sp.wait_ge(S["xw_done"], i * 2 + (u - 1))
                    load_weights(u, i * 2 + u)
                    sp.wait_ge(S["qkv_mm"], i * 2 + (u + 1))
                    load_proj(u, i * 2 + u)

            def load_out(u, e):
                sp.dma_start(w_bc[u], d["w_dram"][bass.ds(e, 1), :].to_broadcast([P, T])).then_inc(S[f"wz_in{u}"], 16)

            def load_out_w(u, e):
                sp.dma_start(o_w[u], d["p_o"][e]).then_inc(S[f"o_in{u}"], 16)

            sp.wait_ge(S["qkv_mm"], E1 + 2)
            for u in range(2):
                load_out(u, u)
                load_out_w(u, u)
            with sp.Fori(1, E1 // 2) as i:
                for u in range(2):
                    sp.wait_ge(S["z_done"], i * 2 + (u - 1))
                    load_out(u, i * 2 + u)
                    sp.wait_ge(S["out_mm"], i * 2 + (u + 1))
                    load_out_w(u, i * 2 + u)
            for b in range(B):
                sp.wait_ge(S["x4_done"], b + 1)
                sp.dma_start(d["out"][b], x[:, b, :]).then_inc(S["out_stored"], 16)
            sp.wait_ge(S["out_stored"], 16 * B)

        @block.gpsimd
        def _(pool):
            def reduce_all(n, col, op):
                pool.wait_ge(S["max_part"], n)
                pool.partition_all_reduce(scol[:, col + 1:col + 2], scol[:, col:col + 1], P, op)\
                    .then_inc(S["max_all"], 1)

            pool.sem_inc(S["y_free"], 2)
            pool.memset(zero_tile[:, :], 0.0).then_inc(S["zero_tile_set"], 1)
            reduce_all(1, 0, RMAX)
            pool.wait_ge(S["w_abs"], 1)
            pool.partition_all_reduce(wabs[:, 7:12], wabs[:, 0:5], P, RADD).then_inc(S["w_abs_all"], 1)
            pool.wait_ge(S["large_abs"], 1)
            pool.partition_all_reduce(wabs[:, 12:14], wabs[:, 5:7], P, RADD).then_inc(S["w_abs_all"], 1)
            pool.wait_ge(S["thresholds"], 1)

            def below(name):
                i, (p, w, a) = TERN_NAMES.index(name), TERN[name]
                return pool.tensor_scalar(weight(name), raw[0:p, a:a + w], ws[0:p, 1, i:i + 1], None, ALU.is_lt)

            def ternarise(n, name):
                i, (p, w, a) = TERN_NAMES.index(name), TERN[name]
                below(name).then_inc(S["pool_step"], 1)
                pool.wait_ge(S["pool_step"], 2 * n - 1)
                pool.tensor_scalar(raw[0:p, a:a + w], raw[0:p, a:a + w], wabs[0:p, i:i + 1], None, ALU.is_gt)\
                    .then_inc(S["pool_step"], 1)
                pool.wait_ge(S["pool_step"], 2 * n)
                pool.tensor_tensor(weight(name), raw[0:p, a:a + w], weight(name), ALU.subtract)\
                    .then_inc(S["tern_ready"], 1)

            below("f1").then_inc(S["below_done"], 1)
            reduce_all(2, 4, RMAX)
            below("f2").then_inc(S["below_done"], 1)
            ternarise(1, "txt")

            pool.wait_ge(S["q_out"], 4)
            pool.wait_ge(S["tern_ready"], 7)
            for u in range(2):
                pool.memset(v_b[u], 0.0).then_inc(S["v_zeroed"], 1)
            with pool.Fori(0, B // 2) as i:
                for u in range(2):
                    b = i * 2 + u
                    pool.wait_ge(S["scores_mm"], i * 32 + (16 * u + 1))
                    for t in range(2):
                        src = qT[:, t, bass.ds(b * N, N)]
                        pool.tensor_tensor(q_b[u][:, 8 * t:8 * t + 8, :],
                                           src[:, None, :].to_broadcast([P, 8, N]),
                                           const("headmask")[:, :, None].to_broadcast([P, 8, N]),
                                           ALU.mult).then_inc(S["q_spread"], 1)

            reduce_all(3, 8, RMAX)
            pool.wait_ge(S["zero_tile_set"], 1)
            for t in range(TILES + 2):
                pool.dma_start(d["x_slots"][t * SLOTS:(t + 1) * SLOTS, :], zero_tile[:, :])\
                    .then_inc(S["zeroed"], 16)
            pool.wait_ge(S["zeroed"], 16 * (TILES + 2))
            pool.wait_ge(S["slot_done"], 1)
            for b in range(B):
                pool.indirect_dma_start(out=d["x_slots"], out_offset=bass.IndirectOffsetOnAxis(
                    ap=slot_of[:, b:b + 1], axis=0), in_=xn[:, b, :], in_offset=None).then_inc(S["scattered"], 16)
            pool.wait_ge(S["scattered"], 16 * B)

            def load_tile(u, t):
                pool.dma_start(xs[u], d["x_slots"][bass.ds(t * SLOTS, SLOTS), :]).then_inc(S[f"xs_in{u}"], 16)

            load_tile(0, 0)
            load_tile(1, 1)
            with pool.Fori(0, TILES // 2) as i:
                for u in range(2):
                    t = i * 2 + u
                    pool.wait_ge(S["xs_turned"], i * 2 + (u + 1))
                    load_tile(u, i * 2 + (u + 2))
                    pool.wait_ge(S["y_out"], i * 2 + (u + 3))
                    pool.dma_start(d["y_slots"][bass.ds(t * SLOTS, SLOTS), :], ys[u])\
                        .then_inc(S[f"y_stored{u}"], 16)
                    pool.wait_ge(S[f"y_stored{u}"], i * 16 + 16)
                    pool.sem_inc(S["y_free"], 1)
            for u in range(2):
                pool.wait_ge(S[f"xs_in{u}"], 16 * (TILES // 2 + 1))
            for b in range(B):
                pool.indirect_dma_start(out=y_tok[:, b, :], out_offset=None, in_=d["y_slots"],
                                        in_offset=bass.IndirectOffsetOnAxis(ap=slot_of[:, b:b + 1], axis=0))\
                    .then_inc(S[f"gathered{b // 2}"], 16)

            reduce_all(4, 12, RMAX)
            reduce_all(5, 16, RMAX)
            reduce_all(6, 20, RMAX)

        @block.vector
        def _(dve):
            steps = [0]

            def link(ins):
                steps[0] += 1
                ins.then_inc(S["dve_step"], 1)
                dve.wait_ge(S["dve_step"], steps[0])

            def token_stats(b):
                return dve.bn_stats(stats[:, b, :], x[:, b, :])

            def layernorm(k, last_stats):
                link(last_stats)
                for b in range(B):
                    ins = dve.bn_aggr(mv[:, b, :], stats[:, b, :])
                link(ins)
                dve.tensor_scalar(var[:, :], mv[:, :, 1], EPS, None, ALU.add).then_inc(S["ln_var"], 1)
                dve.wait_ge(S["ln_std"], k)
                link(dve.reciprocal(rstd[:, :], std[:, :]))
                for b in range(B):
                    dve.tensor_scalar(xn[:, b, :], x[:, b, :], mv[:, b, 0:1], rstd[:, b:b + 1],
                                      ALU.subtract, ALU.mult).then_inc(S["ln_out"], 1)

            def scale_of(n, col, w):
                dve.wait_ge(S["max_all"], n)
                link(dve.tensor_scalar(scol[:, col + 2:col + 3], scol[:, col + 1:col + 2], 1e-8, 1.0 / 127.0,
                                       ALU.max, ALU.mult))
                link(dve.reciprocal(scol[:, col + 3:col + 4], scol[:, col + 2:col + 3]))
                a = TERN_NAMES.index(w[0])
                link(dve.tensor_scalar(scol[:, 40 + a:40 + a + len(w)], ws[:, 0, a:a + len(w)],
                                       scol[:, col + 2:col + 3], None, ALU.mult))

            def quantise(out, src, tmp, col, p=P):
                link(dve.tensor_scalar(tmp, src, scol[0:p, col + 3:col + 4], MAGIC, ALU.mult, ALU.add))
                return dve.tensor_scalar(out, tmp, MAGIC, None, ALU.subtract)

            dve.sem_inc(S["kv_out"], 6)
            dve.sem_inc(S["turn_out"], 2)
            dve.sem_inc(S["h_out_v"], 8)
            dve.sem_inc(S["y_out"], 2)
            dve.memset(wabs[:, :], 0.0)
            link(dve.memset(scol[:, :], 0.0))
            for i in (3, 4):
                ins = dve.memset(psum[i][:, :], 0.0)
            link(ins)

            def ctx_maximum(h):
                dve.wait_ge(S[f"ctx_half_in{h}"], 16)
                return dve.tensor_reduce(umax[0:KC, h:h + 1], ctx_a[0:KC, :, 4 * h:4 * h + 4], AX.XYZ, ALU.max,
                                         apply_absolute_value=True)

            ctx_maximum(0)
            dve.wait_ge(S["x_in"], 16)
            for b in range(B):
                ins = token_stats(b)
            layernorm(1, ins)
            ins = ctx_maximum(1)
            link(ins)
            dve.tensor_reduce(scol[0:KC, 0:1], umax[0:KC, 0:2], AX.X, ALU.max).then_inc(S["max_part"], 1)
            dve.wait_ge(S["raw_in"], 16 * 5)
            for i, name in enumerate(TERN_NAMES[:5]):
                p, w, a = TERN[name]
                ins = dve.tensor_reduce(wabs[0:p, i:i + 1], raw[0:p, a:a + w], AX.X, ALU.add,
                                        apply_absolute_value=True)
            ins.then_inc(S["w_abs"], 1)

            def thresholds(a, b):
                for i, name in list(enumerate(TERN_NAMES))[a:b]:
                    p, w, _ = TERN[name]
                    ins = dve.tensor_scalar(ws[:, 0, i:i + 1], wabs[:, 7 + i:8 + i], 1.0 / (p * w), 1e-5,
                                            ALU.mult, ALU.max)
                link(ins)
                dve.tensor_scalar(ws[:, 1, a:b], ws[:, 0, a:b], -0.5, None, ALU.mult)
                link(dve.tensor_scalar(wabs[:, a:b], ws[:, 0, a:b], 0.5, None, ALU.mult))

            dve.wait_ge(S["w_abs_all"], 1)
            thresholds(0, 5)

            def above(name):
                i, (p, w, a) = TERN_NAMES.index(name), TERN[name]
                dve.scalar_tensor_tensor(weight(name), raw[0:p, a:a + w], wabs[0:p, i:i + 1],
                                         weight(name), ALU.is_gt, ALU.subtract).then_inc(S["tern_ready"], 1)

            def ternarise(*names):
                for name in names:
                    i, (p, w, a) = TERN_NAMES.index(name), TERN[name]
                    link(dve.tensor_scalar(weight(name), raw[0:p, a:a + w], ws[0:p, 1, i:i + 1], None,
                                           ALU.is_lt))
                    above(name)

            ternarise("d2v", "img", "att0", "att1")

            def layer_maxima(stage_n, dst, col):
                with dve.Fori(0, B // 2) as i:
                    for u in range(2):
                        for m in range(2):
                            dve.wait_ge(S["layer_out"], i * 4 + (16 * stage_n + 2 * u + m + 5))
                            dve.tensor_reduce(umax[:, bass.ds(i * 4 + (2 * u + m), 1)],
                                              dst[:, m, i * 2 + u, :], AX.X, ALU.max, apply_absolute_value=True)\
                                .then_inc(S["unit_max"], 1)
                dve.wait_ge(S["unit_max"], 16 * (stage_n + 1))
                dve.tensor_reduce(scol[:, col:col + 1], umax[:, :], AX.X, ALU.max).then_inc(S["max_part"], 1)

            scale_of(1, 0, ("d2v",))
            quantise(qa[0:KC], ctx_a[0:KC], ctx_a[0:KC], 0, KC).then_inc(S["quantised"], 1)
            dve.wait_ge(S["w_abs_all"], 2)
            thresholds(5, 7)
            dve.sem_inc(S["thresholds"], 1)
            layer_maxima(0, kvT, 4)
            scale_of(2, 4, ("img",))
            quantise(qb, kvT[:, :, :, :], kvT[:, :, :, :], 4).then_inc(S["quantised"], 1)
            for n, name in ((1, "f1"), (2, "f2")):
                dve.wait_ge(S["below_done"], n)
                above(name)
            layer_maxima(1, ctx_a, 8)
            dve.tensor_scalar(avg[:, :, :], avg[:, :, :], 1.0 / M, None, ALU.mult)
            dve.wait_ge(S["tern_ready"], 7)
            dve.wait_ge(S["v_zeroed"], 2)
            with dve.Fori(0, B // 2) as i:
                for u in range(2):
                    for c, (_, rows_c) in enumerate(CH):
                        dve.wait_ge(S["proj_mm"], i * 10 + (5 * u + 3 + c))
                        if c == 0:
                            dve.wait_ge(S["pv_mm"], i * 8 + (4 * u + 1))
                        bank = psum[(2 + c) % 3][0:rows_c, 0:D].rearrange("p (g q w) -> p g q w", q=2, w=HD)
                        dst = v_b[u][0:rows_c, c].rearrange("p (g q) w -> p g q w", q=2)
                        bias = rows[0:rows_c, 0:D].rearrange("p (g q w) -> p g q w", q=2, w=HD)
                        for q in range(2):
                            ins = dve.tensor_tensor(dst[:, :, q, q * HD:(q + 1) * HD], bank[:, :, q, :],
                                                    bias[:, :, q, :], ALU.add)
                        ins.then_inc(S["v_out"], 1)
                    for j in range(H + 2):
                        if j < H:
                            dve.wait_ge(S["scores_mm"], i * 32 + (16 * u + 17 + j + 1))
                            dve.tensor_reduce(nmax[:, u, j:j + 1], psum[(5 + j) % 3][0:N, 0:M], AX.X, ALU.max,
                                              negate=True).then_inc(S["max_out"], 1)
                        if j >= 2:
                            k = j - 2
                            dve.wait_ge(S["turned"], i * 32 + (16 * u + 16 + k + 1))
                            if k % 4 == 0:
                                dve.wait_ge(S["pv_mm"], i * 8 + (4 * u + 4 + k // 4))
                            dve.tensor_copy(probsT[k % 8], psum[3 + k % 2][0:CW, 0:3 * N])\
                                .then_inc(S["turn_out"], 1)

            dve.wait_ge(S["exp_out"], 16 * (B + 1))
            dve.reciprocal(precip[:, :, :], psums[:, :, :]).then_inc(S["norm_a"], 1)
            for n in range(4):
                t, half = n // 2, n % 2
                dve.wait_ge(S["norm_mm"], 2 + n + 1)
                if n == 0:
                    dve.wait_ge(S["o_out"], B + 2)
                dst = qT[:, t, half * HT:(half + 1) * HT]
                dve.tensor_tensor(dst, dst, psum[n][:, 0:HT], ALU.mult).then_inc(S["norm_b"], 1)
            scale_of(3, 8, ("att0", "att1"))
            quantise(qb, ctx_a, ctx_a, 8).then_inc(S["quantised"], 1)
            dve.wait_ge(S["gates_done"], 1)
            for b in range(B + 1):
                if b < B:
                    dve.wait_ge(S["y0_mm"], b + 1)
                    link(dve.tensor_tensor(tmp256[:, b % 2, :], psum[b % 4][0:N, 0:D], rows[0:N, 256:512],
                                           ALU.add))
                    dve.scalar_tensor_tensor(x[:, b, :], tmp256[:, b % 2, :], tg[0:N, 0:1], x[:, b, :],
                                             ALU.mult, ALU.add).then_inc(S["x1_done"], 1)
                if b >= 1:
                    dve.wait_ge(S["x1_done"], b)
                    ins = token_stats(b - 1)
            layernorm(2, ins)

            dve.wait_ge(S["logit_mm"], 1)
            lg8, a8, b8 = lg[:, :, 0:E0], l_a[:, :, 0:E0], l_b[:, :, 0:E0]

            def over_e(t, n=E0):
                return t[:, :, None].to_broadcast([N, B, n])

            def along_b(row, n=E0):
                return row[:, None, :].to_broadcast([N, B, n])

            link(dve.tensor_copy(lg8, psum[0][0:N, 0:B * E0].rearrange("p (b e) -> p b e", b=B)))
            link(dve.tensor_reduce(r_a[:, :], lg8, AX.X, ALU.max))
            dve.tensor_tensor(a8, lg8, over_e(r_a), ALU.subtract).then_inc(S["logit_a"], 1)
            link(dve.tensor_tensor(b8, lg8, over_e(r_a), ALU.is_equal))
            link(dve.tensor_tensor(b8, b8, along_b(const("rev8", N)), ALU.mult))
            link(dve.tensor_reduce(r_b[:, :], b8, AX.X, ALU.max))
            dve.memset(seen[:, 0, :], 0.0)
            link(dve.tensor_tensor(onehot[:, :, :], b8, over_e(r_b), ALU.is_equal))
            for b in range(B):
                ins = dve.tensor_tensor(seen[:, b + 1, :], seen[:, b, :], onehot[:, b, :], ALU.add)
                if b < B - 1:
                    link(ins)
            ins.then_inc(S["onehot_done"], 1)
            dve.wait_ge(S["rank_mm"], 1)
            dve.tensor_copy(rank[:, :, :], psum[1][0:N, 0:B * E0].rearrange("p (b e) -> p b e", b=B))
            link(dve.tensor_copy(count[:, :], psum[2][0:N, 0:E0]))
            link(dve.tensor_tensor(ex_a[:, :, 0:OVER], count[:, :, None].to_broadcast([N, E0, OVER]),
                                   const("bounds", N)[:, None, :].to_broadcast([N, E0, OVER]), ALU.is_gt))
            link(dve.tensor_reduce(extra[:, :], ex_a[:, :, 0:OVER], AX.X, ALU.add))
            link(dve.tensor_tensor(ex_a[:, :, :], extra[:, None, :].to_broadcast([N, E0, E0]),
                                   const("lower", N).rearrange("p (a b) -> p a b", a=E0), ALU.mult))
            link(dve.tensor_reduce(extra_base[:, :], ex_a[:, :, :], AX.X, ALU.add))
            link(dve.tensor_tensor(count[:, :], extra[:, :], extra_base[:, :], ALU.add))
            link(dve.tensor_tensor(ex_a[:, 0:OVER, :], count[:, None, :].to_broadcast([N, OVER, E0]),
                                   const("over", N)[:, :, None].to_broadcast([N, OVER, E0]), ALU.is_le))
            link(dve.tensor_reduce(te[:, :], ex_a[:, 0:OVER, :], AX.X, ALU.add))
            dve.tensor_scalar(tile_expert[0:1, :], te[0:1, :], float(E0 - 1), None, ALU.min)\
                .then_inc(S["te_done"], 1)
            link(dve.tensor_scalar(extra[:, :], extra_base[:, :], float(E0 - 1), float(SLOTS), ALU.add, ALU.mult))
            dve.tensor_tensor(rank[:, :, :], rank[:, :, :], onehot[:, :, :], ALU.mult)
            dve.tensor_tensor(l_b[:, :, 0:E0], onehot[:, :, :], along_b(const("base", N)), ALU.mult)
            link(dve.tensor_tensor(l_c[:, :, 0:E0], onehot[:, :, :], along_b(extra), ALU.mult))
            dve.tensor_reduce(r_a[:, :], rank[:, :, :], AX.X, ALU.add)
            dve.tensor_reduce(r_b[:, :], l_b[:, :, 0:E0], AX.X, ALU.add)
            link(dve.tensor_reduce(r_c[:, :], l_c[:, :, 0:E0], AX.X, ALU.add))
            link(dve.tensor_tensor(r_c[:, :], r_c[:, :], r_b[:, :], ALU.subtract))
            link(dve.scalar_tensor_tensor(r_c[:, :], r_a[:, :], float(SLOTS), r_c[:, :], ALU.is_ge, ALU.mult))
            link(dve.tensor_tensor(r_b[:, :], r_b[:, :], r_a[:, :], ALU.add))
            dve.tensor_tensor(slot_of[:, :], r_b[:, :], r_c[:, :], ALU.add).then_inc(S["slot_done"], 1)
            dve.wait_ge(S["logit_e"], 1)
            link(dve.tensor_reduce(r_a[:, :], a8, AX.X, ALU.add))
            link(dve.reciprocal(top_w[:, :], r_a[:, :]))
            link(dve.tensor_scalar(top_w[:, :], top_w[:, :], tg[0:N, 2:3], None, ALU.mult))

            with dve.Fori(0, B) as b:
                for c, (_, rows_c) in enumerate(CH):
                    dve.wait_ge(S["kv_mm"], b * 3 + (c + 1))
                    for a in range(2):
                        dve.scalar_tensor_tensor(
                            kvt[0:rows_c, c, b, a, :], psum[c][0:rows_c, a * P:(a + 1) * P],
                            scol[0:rows_c, 43 + a:44 + a],
                            rows[0:rows_c, 512 + a * P:512 + (a + 1) * P], ALU.mult, ALU.add)\
                            .then_inc(S["kv_out"], 1)

            with dve.Fori(0, TILES // 2) as i:
                for u in range(2):
                    dve.wait_ge(S["h_mm"], i * 4 + (2 * u + 2))
                    dve.wait_ge(S[f"w2_in{u}"], i * 48 + 48)
                    for m in range(4, 8):
                        dve.tensor_scalar(hsT[u][:, m, :], psum[2 * u + 1][:, (m - 4) * P:(m - 3) * P],
                                          e_b1[u][:, m:m + 1], 0.0, ALU.add, ALU.max).then_inc(S["h_out_v"], 1)
                    dve.wait_ge(S["y_mm"], i * 2 + (u + 1))
                    dve.wait_ge(S["y_free"], i * 2 + (u + 1))
                    dve.tensor_tensor(ys[u], psum[4 + u][:, 0:D], e_b2[u], ALU.add).then_inc(S["y_out"], 1)

            for b in range(B + 1):
                if b < B:
                    dve.wait_ge(S[f"gathered{b // 2}"], 32)
                    dve.scalar_tensor_tensor(x[:, b, :], y_tok[:, b, :], top_w[:, b:b + 1], x[:, b, :],
                                             ALU.mult, ALU.add).then_inc(S["x2_done"], 1)
                if b >= 1:
                    dve.wait_ge(S["x2_done"], b)
                    ins = token_stats(b - 1)
            layernorm(3, ins)

            dve.wait_ge(S["xT_ready"], 12)
            dve.tensor_reduce(scol[:, 12:13], xT[:, :, :], AX.XY, ALU.max, apply_absolute_value=True)\
                .then_inc(S["max_part"], 1)
            scale_of(4, 12, ("txt",))
            quantise(qx.rearrange("p k t -> p (k t)"), xT[:, :, :].rearrange("p k t -> p (k t)"), q_tmp, 12)\
                .then_inc(S["quantised"], 1)
            for a in range(2):
                if a == 0:
                    dve.wait_ge(S["txt_out"], 4)
                else:
                    dve.wait_ge(S["f_done"], B)
                link(dve.tensor_tensor(fsum, fT[:, 0, :], fT[:, 1, :], ALU.add))
                dve.tensor_scalar(fsum, fsum, 1.0 / 16.0, None, ALU.mult).then_inc(S["fsum_done"], 1)
                for n in range(B + 4):
                    if n < B:
                        dve.wait_ge(S["bs_mm"], B * a + n + 1)
                        dve.tensor_reduce(nmax[:, 0, n:n + 1], psum[(B * a + n) % 3][0:N, 0:M], AX.X, ALU.max,
                                          negate=True).then_inc(S["bmax"], 1)
                    if 1 <= n <= B:
                        b = n - 1
                        dve.wait_ge(S["bexp"], B * a + b + 1)
                        link(dve.reciprocal(r_a[:, b:b + 1], psums[:, 0, b:b + 1]))
                        dve.tensor_scalar(bprobs[(B * a + b) % 3], bprobs[(B * a + b) % 3], r_a[:, b:b + 1], None, ALU.mult)\
                            .then_inc(S["bnorm"], 1)
                    if n >= 4:
                        add_out(dve, a, n - 4)
            dve.wait_ge(S["f_done"], 2 * B)
            dve.tensor_reduce(umax[:, 0:1], fT, AX.XY, ALU.max, apply_absolute_value=True)
            link(dve.tensor_reduce(umax[:, 1:2], avg[:, :, :], AX.XY, ALU.max, apply_absolute_value=True))
            dve.tensor_tensor(scol[:, 16:17], umax[:, 0:1], umax[:, 1:2], ALU.max).then_inc(S["max_part"], 1)
            scale_of(5, 16, ("f1",))
            link(quantise(qavg, avg[:, :, :], avg[:, :, :], 16))
            quantise(qx.rearrange("p k t -> p (k t)"), fT.rearrange("p k t -> p (k t)"), q_tmp, 16)\
                .then_inc(S["quantised"], 1)
            for n in range(16):
                m, half = n // 2, n % 2
                dve.wait_ge(S["f1_out"], n + 1)
                ins = dve.tensor_reduce(umax[:, n:n + 1], h1T[:, m, half * HT:(half + 1) * HT], AX.X, ALU.max)
            link(ins)
            dve.tensor_reduce(scol[:, 20:21], umax[:, :], AX.X, ALU.max).then_inc(S["max_part"], 1)
            scale_of(6, 20, ("f2",))
            dve.sem_inc(S["h1_scale"], 1)
            for m in range(8):
                if m in OWN:
                    link(dve.tensor_scalar(h1T[:, m, :], h1T[:, m, :], scol[:, 23:24], None, ALU.mult))
                else:
                    dve.wait_ge(S["h1_scaled"], len([k for k in range(m + 1) if k not in OWN]))
                dve.tensor_scalar(q1T[:, m, :], h1T[:, m, :], MAGIC, MAGIC, ALU.add, ALU.subtract)\
                    .then_inc(S["q1_done"], 1)
            for b in range(B + 1):
                if b < B:
                    dve.wait_ge(S["f2_mm"], b + 1)
                    link(dve.scalar_tensor_tensor(tmp256[:, b % 2, :], psum[b % 4][0:N, 0:D], scol[0:N, 46:47],
                                                  rows[0:N, 768:1024], ALU.mult, ALU.add))
                    dve.scalar_tensor_tensor(x[:, b, :], tmp256[:, b % 2, :], tg[0:N, 1:2], x[:, b, :],
                                             ALU.mult, ALU.add).then_inc(S["x3_done"], 1)
                if b >= 1:
                    dve.wait_ge(S["x3_done"], b)
                    ins = token_stats(b - 1)
            layernorm(4, ins)

            dve.tensor_tensor(simsq[:, :, :], sim[:, :, :], sim[:, :, :], ALU.mult).then_inc(S["simsq_done"], 1)
            dve.wait_ge(S["lg_act"], 1)
            link(dve.tensor_scalar(sig[:, :], sig[:, :], 1.0, None, ALU.add))
            link(dve.reciprocal(sig[:, :], sig[:, :]))
            dve.wait_ge(S["lg_act"], 3)
            dve.tensor_scalar(simn[:, :], simn[:, :], 1e-12, None, ALU.max)
            link(dve.tensor_scalar(nsq[:, :], nsq[:, :], 1e-12, None, ALU.max))
            dve.reciprocal(simn[:, :], simn[:, :])
            link(dve.reciprocal(nsq[:, :], nsq[:, :]))
            dve.wait_ge(S["lg_mm"], 1)
            link(dve.tensor_tensor(lg[:, :, :], psum[0][0:N, 0:B * E1].rearrange("p (b e) -> p b e", b=B),
                                   along_b(simn, E1), ALU.mult))
            link(dve.tensor_tensor(lg[:, :, :], lg[:, :, :], over_e(nsq, E1), ALU.mult))
            link(dve.tensor_tensor(lg[:, :, :], lg[:, :, :], along_b(sig, E1), ALU.subtract))
            link(dve.tensor_scalar(l_a[:, :, :], lg[:, :, :], 0.0, None, ALU.is_gt))
            link(dve.tensor_reduce(r_a[:, :], l_a[:, :, :], AX.X, ALU.add))
            dve.tensor_scalar(r_a[:, :], r_a[:, :], 0.0, None, ALU.is_equal)

            def pick(src, out):
                link(dve.tensor_reduce(r_b[:, :], src[:, :, :], AX.X, ALU.max))
                link(dve.tensor_tensor(l_c[:, :, :], src[:, :, :], over_e(r_b, E1), ALU.is_equal))
                link(dve.tensor_tensor(l_c[:, :, :], l_c[:, :, :], along_b(const("rev16", N), E1), ALU.mult))
                link(dve.tensor_reduce(r_b[:, :], l_c[:, :, :], AX.X, ALU.max))
                link(dve.tensor_tensor(out[:, :, :], l_c[:, :, :], over_e(r_b, E1), ALU.is_equal))

            pick(lg, l_b)
            link(dve.scalar_tensor_tensor(l_d[:, :, :], l_b[:, :, :], -BIG, lg[:, :, :], ALU.mult, ALU.add))
            pick(l_d, l_c2)
            link(dve.tensor_tensor(l_b[:, :, :], l_b[:, :, :], l_c2[:, :, :], ALU.add))
            link(dve.tensor_tensor(l_b[:, :, :], l_b[:, :, :], over_e(r_a, E1), ALU.mult))
            link(dve.tensor_tensor(l_a[:, :, :], l_a[:, :, :], l_b[:, :, :], ALU.max))
            link(dve.tensor_scalar(lg[:, :, :], lg[:, :, :], 0.0, None, ALU.max))
            link(dve.tensor_reduce(r_b[:, :], lg[:, :, :], AX.X, ALU.max))
            dve.tensor_tensor(lg[:, :, :], lg[:, :, :], over_e(r_b, E1), ALU.subtract).then_inc(S["lg_vec"], 1)
            dve.wait_ge(S["lg_act"], 4)
            link(dve.tensor_tensor(lg[:, :, :], lg[:, :, :], l_a[:, :, :], ALU.mult))
            link(dve.tensor_reduce(r_b[:, :], lg[:, :, :], AX.X, ALU.add))
            link(dve.reciprocal(r_b[:, :], r_b[:, :]))
            dve.tensor_tensor(lg[:, :, :], lg[:, :, :], over_e(r_b, E1), ALU.mult).then_inc(S["w_done"], 1)

            for half in range(2):
                dve.wait_ge(S["w0_mm"], half + 1)
                at_h = slice(half * HT, (half + 1) * HT)
                ins = dve.tensor_tensor(x_w[0][:, :, at_h], xT[:, :, at_h],
                                        psum[6 + half][:, None, 0:HT].to_broadcast([P, 2, HT]), ALU.mult)
            ins.then_inc(S["xw_done"], 1)
            dve.wait_ge(S["wb_in1"], 16)
            dve.tensor_tensor(x_w[1], xT[:, :, :], w_bc[1][:, None, :].to_broadcast([P, 2, T]),
                              ALU.mult).then_inc(S["xw_done"], 1)
            with dve.Fori(1, E1 // 2) as i:
                for u in range(2):
                    dve.wait_ge(S[f"wb_in{u}"], i * 16 + 16 * u)
                    dve.wait_ge(S["qkv_mm"], i * 2 + (u + 1))
                    dve.tensor_tensor(x_w[u], xT[:, :, :], w_bc[u][:, None, :].to_broadcast([P, 2, T]),
                                      ALU.mult).then_inc(S["xw_done"], 1)
            dve.wait_ge(S["vt_mm"], 2)
            for g in range(2):
                dve.tensor_copy(v_tok[:, 4 * g:4 * g + 4, :],
                                psum[6 + g][0:N, :].rearrange("p (b h) -> p b h", b=4)).then_inc(S["vt_out"], 1)
            for n in range(B + 2):
                if n < B:
                    dve.wait_ge(S["ls_mm"], n + 1)
                    dve.tensor_reduce(nmax[:, 0, n:n + 1], psum[n % 3][0:N, 0:N], AX.X, ALU.max, negate=True)\
                        .then_inc(S["lmax"], 1)
                if 1 <= n <= B:
                    b = n - 1
                    dve.wait_ge(S["lexp"], b + 1)
                    link(dve.reciprocal(r_a[:, b:b + 1], psums[:, 0, b:b + 1]))
                    dve.tensor_scalar(lprobs[b], lprobs[b], r_a[:, b:b + 1], None, ALU.mult)\
                        .then_inc(S["lnorm"], 1)
                if n >= 2:
                    b = n - 2
                    dve.wait_ge(S["lturned"], b + 1)
                    dve.tensor_copy(lprobsT[b], psum[3 + b % 2][0:N, 0:N]).then_inc(S["lturn_out"], 1)
            for g in range(2):
                dve.wait_ge(S["lpv_mm"], 4 * g + 4)
                dve.tensor_copy(oT[:, g * HT:(g + 1) * HT], psum[5 + g][:, 0:HT]).then_inc(S["o_ready"], 1)
            dve.wait_ge(S["o_ready"], 2)
            with dve.Fori(0, E1 // 2) as i:
                for u in range(2):
                    dve.wait_ge(S[f"wz_in{u}"], i * 16 + 16)
                    dve.wait_ge(S["out_mm"], i * 2 + (u + 1))
                    dve.tensor_tensor(z_w[u], oT, w_bc[u], ALU.mult).then_inc(S["z_done"], 1)
            for b in range(B):
                dve.wait_ge(S["y_turned"], b + 1)
                dve.scalar_tensor_tensor(x[:, b, :], psum[4 + b % 4][0:N, 0:D], tg[0:N, 3:4], x[:, b, :],
                                         ALU.mult, ALU.add).then_inc(S["x4_done"], 1)

        @block.scalar
        def _(act):
            act.dma_start(x[:, :, :], d["x"].rearrange("b n d -> n b d")).then_inc(S["x_in"], 16)
            for name in TERN_NAMES:
                p, w, a = TERN[name]
                act.dma_start(raw[0:p, a:a + w], d["t_" + name])\
                    .then_inc(S["large_in" if name in ("f1", "f2") else "raw_in"], 16)
            act.sem_inc(S["layer_out"], 4)
            act.sem_inc(S["exp_out"], 16)
            act.sem_inc(S["o_out"], 2)
            act.sem_inc(S["h_out_a"], 8)

            def layernorm(k):
                act.wait_ge(S["ln_var"], k)
                act.activation(std[:, :], var[:, :], ACT.Sqrt).then_inc(S["ln_std"], 1)
                for n in range(4):
                    kk, half = n // 2, n % 2
                    act.wait_ge(S["ln_turned"], 4 * (k - 1) + n + 1)
                    act.copy(xT[:, kk, half * HT:(half + 1) * HT], psum[4 + n][:, 0:HT]).then_inc(S["xT_ready"], 1)

            layernorm(1)
            act.wait_ge(S["small_in"], 16 * 5)
            act.mul(cols[:, 24:26], cols[:, 0:2], 0.25).then_inc(S["act_step"], 1)
            act.wait_ge(S["act_step"], 1)
            for n in range(4):
                m, half = n // 2, n % 2
                act.wait_ge(S["q_mm"], n + 1)
                act.activation(qT[:, m, half * HT:(half + 1) * HT], psum[n][:, 0:HT], ACT.Identity,
                               bias=cols[:, 24 + m:25 + m], scale=0.25).then_inc(S["q_out"], 1)
            act.wait_ge(S["large_in"], 32)
            for i, name in ((5, "f1"), (6, "f2")):
                p, w, a = TERN[name]
                ins = act.activation(weight(name), raw[:, a:a + w], ACT.Abs, accum_out=wabs[:, i:i + 1])
            ins.then_inc(S["large_abs"], 1)
            act.activation(tg[:, 0:2], rows[:, 1040:1042], ACT.Tanh)
            act.activation(tg[:, 2:4], rows[:, 1042:1044], ACT.Tanh).then_inc(S["gates_done"], 1)

            def layer_out(stage_n, dst, scale_cols, bias, sums=None):
                act.wait_ge(S["quantised"], stage_n + 1)
                with act.Fori(0, B // 2) as i:
                    for u in range(2):
                        for m in range(2):
                            act.wait_ge(S["layer_mm"], i * 4 + (16 * stage_n + 2 * u + m + 1))
                            summed = {} if sums is None else {"accum_out": sums[:, m, bass.ds(i * 2 + u, 1)]}
                            act.activation(dst[:, m, i * 2 + u, :], psum[4 + 2 * u + m][:, 0:M], ACT.Identity,
                                           bias=cols[:, bias + m:bias + m + 1],
                                           scale=scol[:, scale_cols[m]:scale_cols[m] + 1], **summed)\
                                .then_inc(S["layer_out"], 1)

            layer_out(0, kvT, (40, 40), COLS["d2v"])
            layer_out(1, ctx_a, (41, 41), COLS["img"], sums=avg)

            act.wait_ge(S["tern_ready"], 7)
            with act.Fori(0, B // 2) as i:
                for u in range(2):
                    for m in range(2):
                        act.wait_ge(S["proj_mm"], i * 10 + (5 * u + m + 1))
                        if m == 0:
                            act.wait_ge(S["scores_mm"], i * 32 + (16 * u + 1))
                        act.activation(k_b[u][:, m, :], psum[m][:, 0:M], ACT.Identity,
                                       bias=cols[:, 2 + m:3 + m]).then_inc(S["k_out"], 1)
                    for j in range(H):
                        head = ORDER[j]
                        act.wait_ge(S["max_out"], i * 32 + (16 * u + j + 1))
                        act.wait_ge(S["turned"], i * 32 + (16 * u + 16 + j - 3))
                        act.activation(probs[j % 4], psum[(5 + j) % 3][0:N, 0:M], ACT.Exp,
                                       bias=nmax[:, u, j:j + 1],
                                       accum_out=psums[:, i * 2 + u, head:head + 1]).then_inc(S["exp_out"], 1)
                    act.wait_ge(S["pv_mm"], i * 8 + (4 * u + 9))
                    act.copy(qT[:, :, bass.ds(i * 2 * N + u * N, N)],
                             psum[5 + u][:, 0:2 * N].rearrange("p (k n) -> p k n", k=2)).then_inc(S["o_out"], 1)

            for g in range(2):
                act.wait_ge(S["norm_mm"], g + 1)
                act.copy(sumT[:, g * HT:(g + 1) * HT], psum[6 + g][0:H, 0:HT]).then_inc(S["norm_b2"], 1)
            for n in range(8):
                m, half = n // 2, n % 2
                act.wait_ge(S["h0_mm"], n + 1)
                act.activation(h0T[:, m, half * HT:(half + 1) * HT], psum[4 + n % 4][:, 0:HT], ACT.Relu,
                               bias=cols[:, 4 + m:5 + m]).then_inc(S["h0_out"], 1)
            layernorm(2)
            act.wait_ge(S["logit_a"], 1)
            act.activation(l_a[:, :, 0:E0], l_a[:, :, 0:E0], ACT.Exp).then_inc(S["logit_e"], 1)

            def turn_tile(u, value):
                act.wait_ge(S["xs_turned"], value)
                act.copy(xsT[u], psum[6 + u][:, 0:D].rearrange("p (k s) -> p k s", k=2)).then_inc(S["xs_out"], 1)

            layer_out(2, kvT, (43, 44), COLS["att"])
            turn_tile(0, 1)
            with act.Fori(0, TILES // 2) as i:
                for u in range(2):
                    act.wait_ge(S["h_mm"], i * 4 + (2 * u + 1))
                    act.wait_ge(S[f"w2_in{u}"], i * 48 + 48)
                    for m in range(4):
                        act.activation(hsT[u][:, m, :], psum[2 * u][:, m * P:(m + 1) * P], ACT.Relu,
                                       bias=e_b1[u][:, m:m + 1]).then_inc(S["h_out_a"], 1)
                    turn_tile(1 - u, i * 2 + (u + 2))

            layernorm(3)
            act.wait_ge(S["quantised"], 4)
            for n in range(4):
                m, half = n // 2, n % 2
                act.wait_ge(S["txt_mm"], n + 1)
                act.activation(fT[:, m, half * HT:(half + 1) * HT], psum[n][:, 0:HT], ACT.Identity,
                               bias=cols[:, 14 + m:15 + m], scale=scol[:, 42:43]).then_inc(S["txt_out"], 1)
            for a in range(2):
                for n in range(B + 3):
                    if n >= 3:
                        b = n - 3
                        act.wait_ge(S["bturned"], B * a + b + 1)
                        if B * a + b >= 2:
                            act.wait_ge(S["bpv_mm"], B * a + b - 1)
                        act.copy(bprobsT[b % 2], psum[3 + b % 2][0:CW, 0:3 * N]).then_inc(S["bturn_out"], 1)
                    if n < B:
                        b, slot = n, (B * a + n) % 3
                        act.wait_ge(S["bmax"], B * a + b + 1)
                        if B * a + b >= 3:
                            act.wait_ge(S["bturned"], B * a + b - 2)
                        act.activation(bprobs[slot], psum[slot][0:N, 0:M], ACT.Exp, bias=nmax[:, 0, b:b + 1],
                                       accum_out=psums[:, 0, b:b + 1]).then_inc(S["bexp"], 1)
            act.wait_ge(S["quantised"], 5)
            for n in range(16):
                m, half = n // 2, n % 2
                act.wait_ge(S["f1_mm"], n + 1)
                act.activation(h1T[:, m, half * HT:(half + 1) * HT], psum[4 + n % 4][:, 0:HT], ACT.Relu,
                               bias=cols[:, 16 + m:17 + m], scale=scol[:, 45:46]).then_inc(S["f1_out"], 1)
            act.activation(sig[:, :], rows[0:N, 1024:1040], ACT.Exp, scale=-1.0).then_inc(S["lg_act"], 1)
            act.wait_ge(S["h1_scale"], 1)
            for m in range(8):
                if m not in OWN:
                    act.mul(h1T[:, m, :], h1T[:, m, :], scol[:, 23:24]).then_inc(S["h1_scaled"], 1)
            layernorm(4)
            act.wait_ge(S["ln_out"], 4 * B)
            for b in range(B):
                ins = act.activation(square[:, b, :], xn[:, b, :], ACT.Square, accum_out=nsq[:, b:b + 1])
            ins.then_inc(S["sq_done"], 1)
            act.wait_ge(S["sq_done"], 1)
            act.activation(nsq[:, :], nsq[:, :], ACT.Sqrt).then_inc(S["lg_act"], 1)
            act.wait_ge(S["simn_mm"], 1)
            act.activation(simn[:, :], psum[1][0:N, 0:E1], ACT.Sqrt).then_inc(S["lg_act"], 1)
            act.wait_ge(S["lg_vec"], 1)
            act.activation(lg[:, :, :], lg[:, :, :], ACT.Exp).then_inc(S["lg_act"], 1)
            for g in range(2):
                act.wait_ge(S["wT_mm"], g + 1)
                act.copy(wT[:, g * HT:(g + 1) * HT], psum[2 + g][0:E1, 0:HT]).then_inc(S["wT_out"], 1)
            act.wait_ge(S["qkv_mm"], E1 + 2)
            for j in range(3):
                for half in range(2):
                    act.activation(qkvT[j][:, half * HT:(half + 1) * HT], psum[2 * j + half][:, 0:HT], ACT.Copy,
                                   scale=float(HE) ** -0.5 if j == 0 else 1.0).then_inc(S["qkv_out"], 1)
            for b in range(B):
                act.wait_ge(S["lmax"], b + 1)
                act.activation(lprobs[b], psum[b % 3][0:N, 0:N], ACT.Exp, bias=nmax[:, 0, b:b + 1],
                               accum_out=psums[:, 0, b:b + 1]).then_inc(S["lexp"], 1)
            act.wait_ge(S["out_mm"], E1 + 2)
            for m in range(2):
                for half in range(2):
                    act.copy(yT[:, m, half * HT:(half + 1) * HT], psum[2 * m + half][:, 0:HT])\
                        .then_inc(S["yT_out"], 1)

        @block.tensor
        def _(pe):
            pe.sem_inc(S["qkv_mm"], 2)
            pe.sem_inc(S["out_mm"], 2)
            pe.sem_inc(S["scores_mm"], 17)
            pe.sem_inc(S["turned"], 16)
            pe.sem_inc(S["pv_mm"], 5)

            def turn_tokens(k):
                for n in range(4):
                    kk, half = n // 2, n % 2
                    for g in range(4):
                        b = 4 * half + g
                        pe.wait_ge(S["ln_out"], B * (k - 1) + b + 1)
                        ins = pe.transpose(psum[4 + n][:, g * N:(g + 1) * N], xn[:, b, kk * P:(kk + 1) * P],
                                           ident[0:N, 0:N])
                    ins.then_inc(S["ln_turned"], 1)

            def layer(bank, w, src, halves, kk, start=True, stop=True):
                for k in range(kk):
                    ins = pe.matmul(bank, w(k), src(k), start=start and k == 0, stop=stop and k == kk - 1)
                return ins

            pe.wait_ge(S["small_in"], 16 * 5)
            turn_tokens(1)
            pe.wait_ge(S["xT_ready"], 4)
            for n in range(4):
                m, half = n // 2, n % 2
                layer(psum[n][:, 0:HT], lambda k: w_q[:, k, m * P:(m + 1) * P],
                      lambda k: xT[:, k, half * HT:(half + 1) * HT], 2, 2).then_inc(S["q_mm"], 1)

            def context_layer(stage_n, w, src, values=False):
                pe.wait_ge(S["quantised"], stage_n + 1)
                with pe.Fori(0, B // 2) as i:
                    for u in range(2):
                        for m in range(2):
                            pe.wait_ge(S["layer_out"], i * 4 + (16 * stage_n + 2 * u + m + 1))
                            for k in range(2):
                                ins = pe.matmul(psum[4 + 2 * u + m][:, 0:M], w(k, m), src[:, k, i * 2 + u, :],
                                                start=k == 0, stop=k == 1)
                            ins.then_inc(S["layer_mm"], 1)
                        for c, (c0, rows_c) in enumerate(CH if values else ()):
                            pe.wait_ge(S["kv_out"], i * 12 + (6 * u + 2 * c + 2))
                            for k in range(2):
                                ins = pe.matmul(psum[c][0:rows_c, 0:D], qb[:, k, i * 2 + u, c0:c0 + rows_c],
                                                wkv[:, k], start=k == 0, stop=k == 1)
                            ins.then_inc(S["kv_mm"], 1)

            def ternary(name, n):
                w = weight(name).rearrange("p (k n) -> p k n", n=n)
                return w

            wd, wi = ternary("d2v", D), ternary("img", D)
            wa = [ternary("att0", P), ternary("att1", P)]
            a0 = TERN["att0"][2]
            wkv = tern[:, a0:a0 + 512].rearrange("p (a k n) -> p k a n", a=2, k=2)
            context_layer(0, lambda k, m: wd[:, k, m * P:(m + 1) * P], qa[0:KC])
            context_layer(1, lambda k, m: wi[:, k, m * P:(m + 1) * P], qb)
            pe.wait_ge(S["q_out"], 4)
            pe.wait_ge(S["layer_out"], 36)

            def project_keys(i, u, m):
                pe.wait_ge(S[f"ctx_in{u}"], i * 16 + 16)
                pe.wait_ge(S["exp_out"], i * 32 + (16 * u + 14 + m))
                for k in range(2):
                    ins = pe.matmul(psum[m][:, 0:M], w_k[:, k, m * P:(m + 1) * P], ctx_b[u][:, k, :],
                                    start=k == 0, stop=k == 1)
                ins.then_inc(S["proj_mm"], 1)

            def attend(i, u, more):
                for c, (c0, rows_c) in enumerate(CH):
                    if c == 0:
                        pe.wait_ge(S["exp_out"], i * 32 + (16 * u + 16))
                    else:
                        pe.wait_ge(S["k_out"], i * 4 + (2 * u + c))
                    for k in range(2):
                        ins = pe.matmul(psum[(2 + c) % 3][0:rows_c, 0:D], ctx_b[u][:, k, c0:c0 + rows_c],
                                        w_v[:, k, :], start=k == 0, stop=k == 1)
                    ins.then_inc(S["proj_mm"], 1)
                pe.wait_ge(S["q_spread"], i * 4 + (2 * u + 2))
                for j in range(H + 3):
                    if j < H:
                        if j < 3:
                            pe.wait_ge(S["v_out"], i * 6 + (3 * u + j + 1))
                        else:
                            pe.wait_ge(S["exp_out"], i * 32 + (16 * u + 16 + j - 2))
                        head = ORDER[j]
                        pe.matmul(psum[(5 + j) % 3][0:N, 0:M], q_b[u][:, head, :], k_b[u][:, head // 8, :],
                                  start=True, stop=True).then_inc(S["scores_mm"], 1)
                    if j > H and more:
                        project_keys(i + u, 1 - u, j - H - 1)
                    if 2 <= j < H + 2:
                        k = j - 2
                        pe.wait_ge(S["exp_out"], i * 32 + (16 * u + 16 + k + 1))
                        pe.wait_ge(S["turn_out"], i * 32 + (16 * u + k + 1))
                        for c, (c0, rows_c) in enumerate(CH):
                            ins = pe.transpose(psum[3 + k % 2][0:rows_c, c * N:(c + 1) * N],
                                               probs[k % 4][:, c0:c0 + rows_c], ident[0:N, 0:N])
                        ins.then_inc(S["turned"], 1)
                    if j >= 6 and j % 4 == 2:
                        g4 = (j - 6) // 4
                        values(pe, i, u, g4)

            for m in range(2):
                project_keys(0, 0, m)
            with pe.Fori(0, B // 2 - 1) as i:
                for u in range(2):
                    attend(i, u, True)
            attend(B // 2 - 1, 0, True)
            attend(B // 2 - 1, 1, False)

            pe.wait_ge(S["norm_a"], 1)
            pe.wait_ge(S["o_out"], B + 2)
            for g in range(2):
                for n in range(4):
                    ins = pe.transpose(psum[6 + g][0:H, n * N:(n + 1) * N], precip[:, 4 * g + n, :],
                                       ident[0:N, 0:N])
                ins.then_inc(S["norm_mm"], 1)
            pe.wait_ge(S["norm_b2"], 2)
            for n in range(4):
                t, half = n // 2, n % 2
                pe.matmul(psum[n][:, 0:HT], const("spread", H)[:, t * P:(t + 1) * P],
                          sumT[:, half * HT:(half + 1) * HT], start=True, stop=True).then_inc(S["norm_mm"], 1)
            pe.wait_ge(S["norm_b"], 4)
            pe.wait_ge(S["ffn_in"], 32)
            for n in range(8):
                m, half = n // 2, n % 2
                if n >= 4:
                    pe.wait_ge(S["h0_out"], n - 3)
                layer(psum[4 + n % 4][:, 0:HT], lambda k: w_1[:, k, m * P:(m + 1) * P],
                      lambda k: qT[:, k, half * HT:(half + 1) * HT], 2, 2).then_inc(S["h0_mm"], 1)
            pe.wait_ge(S["h0_out"], 8)
            for b in range(B):
                if b >= 4:
                    pe.wait_ge(S["x1_done"], b - 3)
                layer(psum[b % 4][0:N, 0:D], lambda k: h0T[:, k, b * N:(b + 1) * N],
                      lambda k: w_2[:, k, :], 1, 4).then_inc(S["y0_mm"], 1)
            turn_tokens(2)

            pe.wait_ge(S["xT_ready"], 8)
            for b in range(B):
                ins = layer(psum[0][0:N, b * E0:(b + 1) * E0], lambda k: xT[:, k, b * N:(b + 1) * N],
                            lambda k: w_r[:, k, :], 1, 2)
            ins.then_inc(S["logit_mm"], 1)
            pe.wait_ge(S["onehot_done"], 1)
            oh = onehot[:, :, :].rearrange("p b e -> p (b e)")
            before = seen[:, 0:B, :].rearrange("p b e -> p (b e)")
            ones = const("ones", N)[:, 0:N]
            pe.matmul(psum[2][0:N, 0:E0], ones, seen[:, B, :], start=True, stop=True)
            pe.matmul(psum[1][0:N, 0:B * E0], const("before", N), oh, start=True, stop=False)
            pe.matmul(psum[1][0:N, 0:B * E0], ones, before, start=False, stop=True).then_inc(S["rank_mm"], 1)
            pe.wait_ge(S["slot_done"], 1)

            context_layer(2, lambda k, m: wa[m][:, k, :], qb, values=True)
            pe.wait_ge(S["kv_out"], 6 * (B + 1))
            pe.wait_ge(S["layer_out"], 52)

            def turn_tile(u):
                for k in range(2):
                    ins = pe.transpose(psum[6 + u][:, k * P:(k + 1) * P], xs[u][:, k * P:(k + 1) * P], ident)
                ins.then_inc(S["xs_turned"], 1)

            pe.wait_ge(S["xs_in0"], 16)
            turn_tile(0)
            with pe.Fori(0, TILES // 2) as i:
                for u in range(2):
                    pe.wait_ge(S[f"w1_in{u}"], i * 16 + 16)
                    pe.wait_ge(S["xs_out"], i * 2 + (u + 1))
                    for m in range(KF):
                        if m == 0:
                            pe.wait_ge(S["h_out_a"], i * 8 + (4 * u + 4))
                        if m == 4:
                            pe.wait_ge(S["h_out_v"], i * 8 + (4 * u + 4))
                        for k in range(2):
                            ins = pe.matmul(psum[2 * u + m // 4][:, (m % 4) * P:(m % 4 + 1) * P],
                                            e_w1[u][:, k, m * P:(m + 1) * P], xsT[u][:, k, :],
                                            start=k == 0, stop=k == 1)
                        if m % 4 == 3:
                            ins.then_inc(S["h_mm"], 1)
                    pe.wait_ge(S[f"xs_in{1 - u}"], i * 16 + (16 if u == 0 else 32))
                    turn_tile(1 - u)
                    pe.wait_ge(S[f"w2_in{u}"], i * 48 + 48)
                    pe.wait_ge(S["y_out"], i * 2 + (u + 1))
                    for m in range(KF):
                        if m % 4 == 0:
                            pe.wait_ge(S["h_out_a" if m == 0 else "h_out_v"], i * 8 + (4 * u + 12))
                        ins = pe.matmul(psum[4 + u][:, 0:D], hsT[u][:, m, :], e_w2[u][:, m, :],
                                        start=m == 0, stop=m == KF - 1)
                    ins.then_inc(S["y_mm"], 1)
            pe.wait_ge(S["y_out"], TILES + 2)
            pe.wait_ge(S["xs_out"], TILES + 1)

            turn_tokens(3)
            pe.wait_ge(S["quantised"], 4)
            wt = ternary("txt", D)
            for n in range(4):
                m, half = n // 2, n % 2
                layer(psum[n][:, 0:HT], lambda k: wt[:, k, m * P:(m + 1) * P],
                      lambda k: qx[:, k, half * HT:(half + 1) * HT], 2, 2).then_inc(S["txt_mm"], 1)
            for a in range(2):
                pe.wait_ge(S["fsum_done"], a + 1)
                pe.wait_ge(S["xT_ready"], 12)
                for n in range(B + 4):
                    if n < B:
                        if B * a + n >= 3:
                            pe.wait_ge(S["bexp"], B * a + n - 2)
                        pe.matmul(psum[(B * a + n) % 3][0:N, 0:M], fsum[:, n * N:(n + 1) * N], kvT[:, a, n, :],
                                  start=True, stop=True).then_inc(S["bs_mm"], 1)
                    if 2 <= n <= B + 1:
                        b = n - 2
                        pe.wait_ge(S["bnorm"], B * a + b + 1)
                        if B * a + b >= 2:
                            pe.wait_ge(S["bturn_out"], B * a + b - 1)
                        for c, (c0, rows_c) in enumerate(CH):
                            ins = pe.transpose(psum[3 + b % 2][0:rows_c, c * N:(c + 1) * N],
                                               bprobs[(B * a + b) % 3][:, c0:c0 + rows_c], ident[0:N, 0:N])
                        ins.then_inc(S["bturned"], 1)
                    if n >= 4:
                        b = n - 4
                        pe.wait_ge(S["bturn_out"], B * a + b + 1)
                        if B * a + b >= 2:
                            pe.wait_ge(S["f_done"], B * a + b - 1)
                        for c, (c0, rows_c) in enumerate(CH):
                            ins = pe.matmul(psum[5 + b % 2][:, 0:N], kvt[0:rows_c, c, b, a, :],
                                            bprobsT[b % 2][0:rows_c, c * N:(c + 1) * N],
                                            start=c == 0, stop=c == 2)
                        ins.then_inc(S["bpv_mm"], 1)
            pe.wait_ge(S["quantised"], 5)
            pe.wait_ge(S["f_done"], 2 * B)
            wf1, wf2 = ternary("f1", BIT_F), ternary("f2", D)
            for n in range(16):
                m, half = n // 2, n % 2
                if n >= 4:
                    pe.wait_ge(S["f1_out"], n - 3)
                bank = psum[4 + n % 4][:, 0:HT]
                for k in range(2):
                    pe.matmul(bank, wf1[:, k, m * P:(m + 1) * P], qx[:, k, half * HT:(half + 1) * HT],
                              start=k == 0, stop=False)
                for k in range(2):
                    ins = pe.matmul(bank, wf1[:, 2 + k, m * P:(m + 1) * P],
                                    qavg[:, k, 4 * half:4 * half + 4, None].to_broadcast([P, 4, N]),
                                    start=False, stop=k == 1)
                ins.then_inc(S["f1_mm"], 1)
            for b in range(B):
                if b >= 4:
                    pe.wait_ge(S["x3_done"], b - 3)
                for k in range(8):
                    if b == 0:
                        pe.wait_ge(S["q1_done"], k + 1)
                    ins = pe.matmul(psum[b % 4][0:N, 0:D], q1T[:, k, b * N:(b + 1) * N], wf2[:, k, :],
                                    start=k == 0, stop=k == 7)
                ins.then_inc(S["f2_mm"], 1)
            turn_tokens(4)

            pe.wait_ge(S["xT_ready"], 16)
            for b in range(B):
                ins = layer(psum[0][0:N, b * E1:(b + 1) * E1], lambda k: xT[:, k, b * N:(b + 1) * N],
                            lambda k: sim[:, k, :], 1, 2)
            ins.then_inc(S["lg_mm"], 1)
            pe.wait_ge(S["simsq_done"], 1)
            layer(psum[1][0:N, 0:E1], lambda k: const("ones")[:, 0:N], lambda k: simsq[:, k, :], 1, 2)\
                .then_inc(S["simn_mm"], 1)
            pe.wait_ge(S["w_done"], 1)
            for g in range(2):
                for n in range(4):
                    ins = pe.transpose(psum[2 + g][0:E1, n * N:(n + 1) * N], lg[:, 4 * g + n, :],
                                       ident[0:N, 0:N])
                ins.then_inc(S["wT_mm"], 1)
            for half in range(2):
                pe.wait_ge(S["wT_out"], half + 1)
                pe.matmul(psum[6 + half][:, 0:HT], const("ones")[0:1, 0:P], wT[0:1, half * HT:(half + 1) * HT],
                          start=True, stop=True).then_inc(S["w0_mm"], 1)

            def project(i, u, first, last):
                pe.wait_ge(S[f"p_in{u}"], i * 16 + 16)
                pe.wait_ge(S["xw_done"], i * 2 + (u + 1))
                for j in range(3):
                    for k in range(2):
                        for half in range(2):
                            ins = pe.matmul(psum[2 * j + half][:, 0:HT], p_w[u][:, k, j * HE:(j + 1) * HE],
                                            x_w[u][:, k, half * HT:(half + 1) * HT],
                                            start=first and k == 0, stop=last and k == 1)
                ins.then_inc(S["qkv_mm"], 1)

            project(0, 0, True, False)
            project(0, 1, False, False)
            with pe.Fori(1, E1 // 2 - 1) as i:
                for u in range(2):
                    project(i, u, False, False)
            project(E1 // 2 - 1, 0, False, False)
            project(E1 // 2 - 1, 1, False, True)
            pe.wait_ge(S["qkv_out"], 6)
            for g in range(2):
                for n in range(4):
                    b = 4 * g + n
                    ins = pe.transpose(psum[6 + g][0:N, n * HE:(n + 1) * HE], qkvT[2][:, b * N:(b + 1) * N],
                                       ident)
                ins.then_inc(S["vt_mm"], 1)
            for n in range(B + 2):
                if n < B:
                    if n >= 3:
                        pe.wait_ge(S["lexp"], n - 2)
                    pe.matmul(psum[n % 3][0:N, 0:N], qkvT[0][:, n * N:(n + 1) * N],
                              qkvT[1][:, n * N:(n + 1) * N], start=True, stop=True).then_inc(S["ls_mm"], 1)
                if 1 <= n <= B:
                    b = n - 1
                    pe.wait_ge(S["lnorm"], b + 1)
                    if b >= 2:
                        pe.wait_ge(S["lturn_out"], b - 1)
                    pe.transpose(psum[3 + b % 2][0:N, 0:N], lprobs[b], ident[0:N, 0:N]).then_inc(S["lturned"], 1)
                if n >= 2:
                    b = n - 2
                    if b == 0:
                        pe.wait_ge(S["vt_out"], 2)
                    pe.wait_ge(S["lturn_out"], b + 1)
                    pe.matmul(psum[5 + b // 4][:, (b % 4) * N:(b % 4 + 1) * N], v_tok[:, b, :], lprobsT[b],
                              start=True, stop=True).then_inc(S["lpv_mm"], 1)
            pe.wait_ge(S["o_ready"], 2)

            def project_out(i, u, first, last):
                pe.wait_ge(S[f"o_in{u}"], i * 16 + 16)
                pe.wait_ge(S["z_done"], i * 2 + (u + 1))
                for m in range(2):
                    for half in range(2):
                        ins = pe.matmul(psum[2 * m + half][:, 0:HT], o_w[u][:, m * P:(m + 1) * P],
                                        z_w[u][:, half * HT:(half + 1) * HT], start=first, stop=last)
                ins.then_inc(S["out_mm"], 1)

            project_out(0, 0, True, False)
            project_out(0, 1, False, False)
            with pe.Fori(1, E1 // 2 - 1) as i:
                for u in range(2):
                    project_out(i, u, False, False)
            project_out(E1 // 2 - 1, 0, False, False)
            project_out(E1 // 2 - 1, 1, False, True)
            pe.wait_ge(S["yT_out"], 4)
            for b in range(B):
                if b >= 4:
                    pe.wait_ge(S["x4_done"], b - 3)
                for m in range(2):
                    ins = pe.transpose(psum[4 + b % 4][0:N, m * P:(m + 1) * P], yT[:, m, b * N:(b + 1) * N],
                                       ident)
                ins.then_inc(S["y_turned"], 1)


def kernel(x, ctx_768, g_xattn, g_ffn, **w):
    import concourse.bacc as bacc
    from concourse.bass_utils import run_bass_kernel_spmd

    def cut_k(a, p):
        return np.ascontiguousarray(a.reshape(-1, p, a.shape[-1]).swapaxes(0, 1))

    w = {k: np.asarray(v) for k, v in w.items()}
    f = np.float32
    cols = np.concatenate([w[n].reshape(-1, P).T for n in (
        "L0_xattn_bq", "L0_xattn_bk", "L0_xattn_b1", "L1_xattn_b_d2v", "L1_xattn_b_img", "L1_xattn_b_att0",
        "L1_xattn_b_att1", "L1_xattn_b_txt", "L1_xattn_b_f1")], axis=1)
    rows = np.concatenate([np.asarray(a).reshape(-1) for a in (
        w["L0_xattn_bv"], w["L0_xattn_b2"], w["L1_xattn_b_att0"], w["L1_xattn_b_att1"], w["L1_xattn_b_f2"],
        w["L1_ffn_gates"], g_xattn, g_ffn)])[None]
    w_a = np.zeros((P, 1552), f)
    w_a[:, 0:512] = cut_k(w["L0_xattn_Wq"], P).reshape(P, -1)
    w_a[0:KC, 512:1024] = cut_k(w["L0_xattn_Wk"], KC).reshape(KC, -1)
    w_a[0:KC, 1024:1536] = cut_k(w["L0_xattn_Wv"], KC).reshape(KC, -1)
    w_a[:, 1536:1552] = cut_k(w["L0_ffn_w_router"], P).reshape(P, -1)
    ctx = np.asarray(ctx_768)
    arrays = {
        "consts": shape_constants(),
        "cols": cols,
        "rows": rows,
        "w_a": w_a,
        "x": np.asarray(x),
        "ctxT": ctx.transpose(2, 0, 1).reshape(2, KC, B, M).transpose(1, 0, 2, 3),
        "w_1": cut_k(w["L0_xattn_W1"], P),
        "w_2": cut_k(w["L0_xattn_W2"], P),
        "e_w1": w["L0_ffn_w1"].reshape(E0, 2, P, FE).transpose(0, 2, 1, 3),
        "e_w2": w["L0_ffn_w2"].reshape(E0, KF, P, D).transpose(0, 2, 1, 3),
        "e_b1": w["L0_ffn_b1"].reshape(E0, KF, P).transpose(0, 2, 1),
        "e_b2": w["L0_ffn_b2"],
        "t_d2v": cut_k(w["L1_xattn_W_d2v"].T, KC).reshape(KC, -1),
        "t_img": cut_k(w["L1_xattn_W_img"].T, P).reshape(P, -1),
        "t_txt": cut_k(w["L1_xattn_W_txt"].T, P).reshape(P, -1),
        "t_att0": cut_k(w["L1_xattn_W_att0"].T, P).reshape(P, -1),
        "t_att1": cut_k(w["L1_xattn_W_att1"].T, P).reshape(P, -1),
        "t_f1": cut_k(w["L1_xattn_W_f1"].T, P).reshape(P, -1),
        "t_f2": cut_k(w["L1_xattn_W_f2"].T, P).reshape(P, -1),
        "sim": cut_k(w["L1_ffn_sim_matrix"], P),
        "p_qkv": np.concatenate([w["L1_ffn_q_proj"], w["L1_ffn_k_proj"], w["L1_ffn_v_proj"]], axis=2)
                   .reshape(E1, 2, P, 3 * HE).transpose(0, 2, 1, 3),
        "p_o": w["L1_ffn_o_proj"],
    }
    arrays = {k: np.ascontiguousarray(v) for k, v in arrays.items()}
    nc = bacc.Bacc("TRN2", target_bir_lowering=False, num_devices=1)
    dram = {k: nc.dram_tensor("in_" + k, v.shape, mybir.dt.from_np(v.dtype), kind="ExternalInput").ap()
            for k, v in arrays.items()}
    dram["x_slots"] = nc.dram_tensor("x_slots", ((TILES + 2) * SLOTS, D), F32).ap()
    dram["y_slots"] = nc.dram_tensor("y_slots", (TILES * SLOTS, D), F32).ap()
    dram["w_dram"] = nc.dram_tensor("w_dram", (E1, T), F32).ap()
    dram["out"] = nc.dram_tensor("out", (B, N, D), F32, kind="ExternalOutput").ap()
    flamingo(nc, dram)
    r = run_bass_kernel_spmd(nc, [{"in_" + k: v for k, v in arrays.items()}], core_ids=[0])
    return r.results[0]["out"]
```
